# Optimizing a Trainium2 kernel written in Bass

```python
import numpy as np
import jax
import jax.numpy as jnp

def _softmax(x, axis=-1):
    return jax.nn.softmax(x, axis=axis)

def _gelu(x):
    return jax.nn.gelu(x, approximate=True)

def _silu(x):
    return jax.nn.silu(x)

def _sigmoid(x):
    return jax.nn.sigmoid(x)

def _layernorm(x, axis=-1, eps=1e-05):
    m = jnp.mean(x, axis=axis, keepdims=True)
    v = jnp.var(x, axis=axis, keepdims=True)
    return (x - m) / jnp.sqrt(v + eps)

def _scatter_add(tgt, idx, src, axis=0):
    return tgt.at[idx].add(src)

def _segment_sum(src, seg, n):
    return jax.ops.segment_sum(src, seg, n)
kernel_name = 'mk_seq_postln_d1_jaxref_r8_4ea00f'

def setup_inputs(seed: int=0):
    np.random.seed(seed)
    _w = jnp.asarray

    def _L0_attn_setup():
        import jax, jax.numpy as jnp
        import numpy as np
        B_, L_, D_, E_, N_, R_, K_ = (2, 256, 256, 512, 16, 128, 4)
        key = jax.random.key(seed)
        ks = jax.random.split(key, 12)
        s = lambda k, shape, scale: jax.random.normal(k, shape, dtype=jnp.float32) * scale
        return {'resid': s(ks[0], (B_, L_, D_), 1.0), 'norm_w': jnp.ones((D_,), jnp.float32), 'W_skip': s(ks[1], (E_, D_), D_ ** (-0.5)), 'W_in': s(ks[2], (E_, D_), D_ ** (-0.5)), 'conv_w': s(ks[3], (E_, 1, K_), K_ ** (-0.5)), 'conv_b': s(ks[4], (E_,), 0.02), 'W_d1': s(ks[5], (R_, E_), E_ ** (-0.5)), 'W_d2': s(ks[6], (E_, R_), R_ ** (-0.5)), 'b_d2': s(ks[7], (E_,), 0.02) - 2.0, 'W_Bm': s(ks[8], (N_, E_), E_ ** (-0.5)), 'W_Cm': s(ks[9], (N_, E_), E_ ** (-0.5)), 'A_log': s(ks[10], (E_, N_), 0.5), 'W_D': jnp.ones((E_,), jnp.float32), 'W_out': s(ks[11], (D_, E_), E_ ** (-0.5))}
    _L0_attn_in = _L0_attn_setup()

    def _L0_ffn_setup():
        import jax, jax.numpy as jnp
        import numpy as np
        B, L, D = (2, 128, 256)
        E, K = (8, 2)
        H, HS = (176, 352)
        key = jax.random.key(seed)
        ks = jax.random.split(key, 9)
        s = 0.02
        return {'x': jax.random.normal(ks[0], (B, L, D), dtype=jnp.float32), 'gate_w': jax.random.normal(ks[1], (E, D), dtype=jnp.float32) * s, 'w_gate': jax.random.normal(ks[2], (E, D, H), dtype=jnp.float32) * s, 'w_up': jax.random.normal(ks[3], (E, D, H), dtype=jnp.float32) * s, 'w_down': jax.random.normal(ks[4], (E, H, D), dtype=jnp.float32) * s, 'shgate_w': jax.random.normal(ks[5], (D,), dtype=jnp.float32) * s, 'shw_gate': jax.random.normal(ks[6], (D, HS), dtype=jnp.float32) * s, 'shw_up': jax.random.normal(ks[7], (D, HS), dtype=jnp.float32) * s, 'shw_down': jax.random.normal(ks[8], (HS, D), dtype=jnp.float32) * s}
    _L0_ffn_in = _L0_ffn_setup()
    _d = {'L0_attn_resid': _L0_attn_in['resid'], 'L0_attn_norm_w': _L0_attn_in['norm_w'], 'L0_attn_W_skip': _L0_attn_in['W_skip'], 'L0_attn_W_in': _L0_attn_in['W_in'], 'L0_attn_conv_w': _L0_attn_in['conv_w'], 'L0_attn_conv_b': _L0_attn_in['conv_b'], 'L0_attn_W_d1': _L0_attn_in['W_d1'], 'L0_attn_W_d2': _L0_attn_in['W_d2'], 'L0_attn_b_d2': _L0_attn_in['b_d2'], 'L0_attn_W_Bm': _L0_attn_in['W_Bm'], 'L0_attn_W_Cm': _L0_attn_in['W_Cm'], 'L0_attn_A_log': _L0_attn_in['A_log'], 'L0_attn_W_D': _L0_attn_in['W_D'], 'L0_attn_W_out': _L0_attn_in['W_out'], 'L0_ffn_gate_w': _L0_ffn_in['gate_w'], 'L0_ffn_w_gate': _L0_ffn_in['w_gate'], 'L0_ffn_w_up': _L0_ffn_in['w_up'], 'L0_ffn_w_down': _L0_ffn_in['w_down'], 'L0_ffn_shgate_w': _L0_ffn_in['shgate_w'], 'L0_ffn_shw_gate': _L0_ffn_in['shw_gate'], 'L0_ffn_shw_up': _L0_ffn_in['shw_up'], 'L0_ffn_shw_down': _L0_ffn_in['shw_down']}
    _x0 = _d['L0_attn_resid']
    _d['L0_attn_resid'] = jax.random.normal(jax.random.fold_in(jax.random.key(seed), 1), (16, 256, 256), dtype=_x0.dtype)
    del _x0
    return _d

def reference(L0_attn_resid, L0_attn_norm_w, L0_attn_W_skip, L0_attn_W_in, L0_attn_conv_w, L0_attn_conv_b, L0_attn_W_d1, L0_attn_W_d2, L0_attn_b_d2, L0_attn_W_Bm, L0_attn_W_Cm, L0_attn_A_log, L0_attn_W_D, L0_attn_W_out, L0_ffn_gate_w, L0_ffn_w_gate, L0_ffn_w_up, L0_ffn_w_down, L0_ffn_shgate_w, L0_ffn_shw_gate, L0_ffn_shw_up, L0_ffn_shw_down):

    def _L0_attn_ref(resid, norm_w, W_skip, W_in, conv_w, conv_b, W_d1, W_d2, b_d2, W_Bm, W_Cm, A_log, W_D, W_out):
        import jax, jax.numpy as jnp
        import numpy as np
        B_, L_, D_, E_, N_, R_, K_ = (2, 256, 256, 512, 16, 128, 4)
        eps = 1e-05
        E, K = (conv_w.shape[0], conv_w.shape[-1])
        x = resid * jax.lax.rsqrt(jnp.mean(resid * resid, -1, keepdims=True) + eps) * norm_w
        skip = x @ W_skip.T
        x = x @ W_in.T
        xc = jnp.swapaxes(x, 1, 2)
        xc = jax.lax.conv_general_dilated(xc, conv_w, (1,), [(K - 1, 0)], dimension_numbers=('NCH', 'OIH', 'NCH'), feature_group_count=E)
        xc = xc + conv_b[None, :, None]
        x = jax.nn.silu(jnp.swapaxes(xc, 1, 2))
        A = -jnp.exp(A_log)
        delta = jax.nn.softplus(x @ W_d1.T @ W_d2.T + b_d2)
        Bt = x @ W_Bm.T
        Ct = x @ W_Cm.T

        def step(h, inp):
            x_t, d_t, b_t, c_t = inp
            h = jnp.exp(d_t[:, :, None] * A) * h + (d_t * x_t)[:, :, None] * b_t[:, None, :]
            y = jnp.einsum('ben,bn->be', h, c_t)
            return (h, y)
        xs = (jnp.swapaxes(x, 0, 1), jnp.swapaxes(delta, 0, 1), jnp.swapaxes(Bt, 0, 1), jnp.swapaxes(Ct, 0, 1))
        h0 = jnp.zeros((x.shape[0], A.shape[0], A.shape[1]), x.dtype)
        _, ys = jax.lax.scan(step, h0, xs)
        y = jnp.swapaxes(ys, 0, 1)
        y = y + x * W_D
        y = y * jax.nn.silu(skip)
        return resid + y @ W_out.T

    def _L0_ffn_ref(x, gate_w, w_gate, w_up, w_down, shgate_w, shw_gate, shw_up, shw_down):
        import jax, jax.numpy as jnp
        import numpy as np
        B, L, D = (2, 128, 256)
        E, K = (8, 2)
        H, HS = (176, 352)
        b, l, d = x.shape
        xf = x.reshape(-1, d)
        logits = jnp.einsum('td,ed->te', xf.astype(jnp.float32), gate_w)
        probs = jax.nn.softmax(logits.astype(jnp.float32), axis=-1)
        weights, indices = jax.lax.top_k(probs, K)
        weights = (weights / weights.sum(-1, keepdims=True)).astype(x.dtype)
        onehot = jax.nn.one_hot(indices, E, dtype=x.dtype)
        combine = jnp.einsum('tk,tke->te', weights, onehot)
        g = jnp.einsum('td,edh->teh', xf, w_gate)
        u = jnp.einsum('td,edh->teh', xf, w_up)
        h = jax.nn.silu(g) * u
        out = jnp.einsum('teh,ehd,te->td', h.astype(jnp.float32), w_down.astype(jnp.float32), combine.astype(jnp.float32))
        sgate = jax.nn.sigmoid(xf @ shgate_w)[:, None]
        sh = jax.nn.silu(xf @ shw_gate) * (xf @ shw_up) @ shw_down
        out = out + (sgate * sh).astype(jnp.float32)
        return out.astype(x.dtype).reshape(b, l, d)
    x = L0_attn_resid
    x = _layernorm(x + _L0_attn_ref(x, L0_attn_norm_w, L0_attn_W_skip, L0_attn_W_in, L0_attn_conv_w, L0_attn_conv_b, L0_attn_W_d1, L0_attn_W_d2, L0_attn_b_d2, L0_attn_W_Bm, L0_attn_W_Cm, L0_attn_A_log, L0_attn_W_D, L0_attn_W_out), axis=-1)
    x = _layernorm(x + _L0_ffn_ref(x, L0_ffn_gate_w, L0_ffn_w_gate, L0_ffn_w_up, L0_ffn_w_down, L0_ffn_shgate_w, L0_ffn_shw_gate, L0_ffn_shw_up, L0_ffn_shw_down), axis=-1)
    return x

_drawn_inputs = setup_inputs


def setup_inputs(seed=0):
    import zlib

    import numpy as np

    out = dict(_drawn_inputs(seed))
    spreads = {'L0_attn_norm_w': (1.0, 0.2), 'L0_attn_W_D': (1.0, 0.59)}
    factors = {'L0_attn_conv_b': 8.0,
     'L0_attn_b_d2': 64.0,
     'L0_ffn_gate_w': 6.547,
     'L0_ffn_w_gate': 5.756,
     'L0_ffn_w_up': 5.704,
     'L0_ffn_w_down': 5.689,
     'L0_ffn_shgate_w': 8.0,
     'L0_ffn_shw_gate': 5.736,
     'L0_ffn_shw_up': 5.652,
     'L0_ffn_shw_down': 5.648,
     'L0_attn_W_d1': 8.0,
     'L0_attn_W_d2': 8.0,
     'L0_attn_W_Bm': 8.0,
     'L0_attn_W_Cm': 8.0,
     'L0_attn_A_log': 8.0}
    for name, (base, spread) in spreads.items():
        noise = np.random.default_rng([zlib.crc32(name.encode()), seed]).standard_normal(out[name].shape)
        drawn = base * np.exp(spread * noise) if base else spread * noise
        out[name] = jnp.asarray(drawn.astype(out[name].dtype))
    for name, factor in factors.items():
        out[name] = (out[name] * factor).astype(out[name].dtype)
    return out
```

```python
from contextlib import ExitStack

import concourse.bass as bass
from concourse import mybir

ALU = mybir.AluOpType
ACT = mybir.ActivationFunctionType
AX = mybir.AxisListType
F32 = mybir.dt.float32
BF16 = mybir.dt.bfloat16

P = 128
EPS = 1e-5


class Group:

    def __init__(self, base, it=None):
        self.base, self.it = base, it

    def __add__(self, d):
        return Group(self.base + d, self.it)

    def count(self, per, k):
        fixed = self.base * per + k
        return fixed if self.it is None else self.it * (2 * per) + fixed

    def held(self, eng, per, k):
        if self.it is None:
            return self.count(per, k)
        reg = eng.alloc_register()
        eng.reg_mov(reg, self.count(per, k))
        return eng.snap(reg)

    def beyond(self, n):
        return self.base >= n

    def index(self):
        return self.base if self.it is None else self.it * 2 + self.base


def build(nc, resid, w_xin, norm_w, conv_w, conv_b, w_d1, w_d2, b_d2, w_bc, a_log, w_dd, w_out,
          w_router, w_gate, w_up, w_down, sel, tri, ident, out):
    NG, L, D = resid.shape
    TT = L // P
    KD = D // P
    E = w_dd.shape[0] * w_dd.shape[1]
    J = E // P
    NS = a_log.shape[2]
    R = w_d2.shape[0]
    TAPS = conv_w.shape[2]
    NX = w_router.shape[2] - 1
    NXS = NX + 1
    FEAT = w_gate.shape[2]
    FT = (FEAT + P - 1) // P
    FPAIRS = FT // 2
    LAST = FEAT - (FT - 1) * P
    QUAD = 4
    NQ = NS // QUAD
    SLOTS = J * NQ
    PAIRS = 2 * SLOTS
    HRING = 4
    PJ = NS // 2
    assert TT == 2 and KD == 2 and J == 4 and FT == 14 and TAPS == 4 and R == P and NX == 8

    with ExitStack() as ctx:
        def sb(name, shape, dt=F32):
            return ctx.enter_context(nc.sbuf_tensor(name, shape, dt))

        def ps(name, shape, dt=F32):
            return ctx.enter_context(nc.psum_tensor(name, shape, dt))

        def sem(name):
            return ctx.enter_context(nc.semaphore(name))

        wxin = sb("wxin", [P, KD, 2 * E])
        normw = sb("normw", [P, KD])
        convw = sb("convw", [P, J, TAPS])
        convb = sb("convb", [P, J])
        wd1 = sb("wd1", [P, J, R])
        wd2 = sb("wd2", [R, E])
        bd2 = sb("bd2", [P, J])
        wbc = sb("wbc", [P, J, 2 * NS])
        amat = sb("amat", [P, J, NS])
        wdd = sb("wdd", [P, J])
        wout = sb("wout", [P, J, D])
        wrt = sb("wrt", [P, KD, NXS])
        wg = sb("wg", [P, KD, FEAT])
        wu = sb("wu", [P, KD, FEAT])
        wdn = sb("wdn", [P, FT, D])
        selb = sb("selb", [3 * NXS, FEAT], BF16)
        lower = sb("lower", [P, NX, NX])
        idn = sb("idn", [P, P])
        idb = sb("idb", [P, P], BF16)
        eps = sb("eps", [P, 1])

        xr = sb("xr", [P, TT, D])
        sqd = sb("sqd", [P, D])
        ss = sb("ss", [P, TT])
        rms = sb("rms", [P, TT])
        rinv = sb("rinv", [P, TT])
        xn = sb("xn", [P, TT, D])
        xnT = sb("xnT", [P, 2, KD, L])
        xin = sb("xin", [P, J, TAPS - 1 + L])
        cv = sb("cv", [P, J, L])
        xa = sb("xa", [P, 2, J, L])
        r1 = sb("r1", [P, L])
        bcs = sb("bcs", [2 * NS, L])
        spz = sb("spz", [P, J, L])
        spr = sb("spr", [P, J, L])
        spu = sb("spu", [P, J, L])
        dlt = sb("dlt", [P, 2, J, L])
        dx = sb("dx", [P, 2, J, L])
        sk = sb("sk", [P, 2, J, L])

        Bb = sb("Bb", [P, NS, L])
        Cb = sb("Cb", [P, NS, L])
        dbx = sb("dbx", [P, 2, QUAD, L])
        pr = sb("pr", [P, 4, 2, L])
        yTs = sb("yTs", [P, 2, TT, P])
        yd = sb("yd", [P, 2, L])
        yg = sb("yg", [P, J, L])

        x1 = sb("x1", [P, 2, TT, D])
        st1 = sb("st1", [P, TT, 6])
        mv1 = sb("mv1", [P, TT, 2])
        sd1 = sb("sd1", [P, TT])
        ri1 = sb("ri1", [P, TT])
        st2 = sb("st2", [P, TT, 6])
        mv2 = sb("mv2", [P, TT, 2])
        sd2 = sb("sd2", [P, TT])
        ri2 = sb("ri2", [P, TT])
        x1T = sb("x1T", [P, KD, L])
        lmax = sb("lmax", [P, TT])
        ex = sb("ex", [P, TT, NX])
        sgt = sb("sgt", [P, TT, 1])
        gt = sb("gt", [P, TT, NX, NX])
        eq = sb("eq", [P, TT, NX, NX])
        rank = sb("rank", [P, TT, NX])
        top = sb("top", [P, TT, NX])
        tsum = sb("tsum", [P, TT])
        tinv = sb("tinv", [P, TT])
        comb = sb("comb", [P, TT, NXS])
        cpart = sb("cpart", [P, TT, 3, NXS], BF16)
        crest = sb("crest", [P, TT, NXS])
        cT = sb("cT", [3 * NXS, L], BF16)
        hh = sb("hh", [P, HRING, 2, L])
        ob = sb("ob", [P, 2, TT, D])

        bcd = nc.dram_tensor("bc_scratch", [2, 2 * NS, L], F32, kind="Internal").ap()

        dA = [ps(f"dA{i}", [P, 2, L]) for i in range(2)]
        yT = ps("yT", [P, 2, TT, P])
        work = [ps(f"work{i}", [P, 512]) for i in range(2)]
        gps = ps("gps", [P, 2, L])
        ups = ps("ups", [P, 2, L])
        ops = ps("ops", [P, TT, D])

        w_in = sem("w_in")
        wf_in = sem("wf_in")
        prep_act = sem("prep_act")
        prep = sem("prep")
        PREP = 7
        xr_in = sem("xr_in")
        res_in = sem("res_in")
        bc_st = sem("bc_st")
        b_in = [sem(f"b_in{q}") for q in range(NQ)]
        c_in = [sem(f"c_in{q}") for q in range(NQ)]
        out_st = sem("out_st")
        squares = sem("squares")
        rms_root = sem("rms_root")
        rms_inv = sem("rms_inv")
        xn_done = sem("xn_done")
        xnT_ps = sem("xnT_ps")
        xnT_done = sem("xnT_done")
        in_ps = sem("in_ps")
        conv_in = sem("conv_in")
        conv_step = sem("conv_step")
        conv_tanh = sem("conv_tanh")
        xa_done = sem("xa_done")
        d1_ps = sem("d1_ps")
        d1_read = sem("d1_read")
        d2_ps = sem("d2_ps")
        d2_read = sem("d2_read")
        sp_exp = sem("sp_exp")
        sp_ln = sem("sp_ln")
        sp_pool = sem("sp_pool")
        dlt_done = sem("dlt_done")
        dx_done = sem("dx_done")
        skip_ps = sem("skip_ps")
        skip_tanh = sem("skip_tanh")
        sk_done = sem("sk_done")
        dA_full = sem("dA_full")
        dbx_full = sem("dbx_full")
        scan_done = sem("scan_done")
        cmul_dve = sem("cmul_dve")
        cmul_pool = sem("cmul_pool")
        summed = sem("summed")
        yT_copied = sem("yT_copied")
        yb_ps = sem("yb_ps")
        yb_read = sem("yb_read")
        yg_done = sem("yg_done")
        outp_ps = sem("outp_ps")
        res_sum = sem("res_sum")
        ln1_stat = sem("ln1_stat")
        ln1_root = sem("ln1_root")
        ln1_inv = sem("ln1_inv")
        x1_done = sem("x1_done")
        x1T_ps = sem("x1T_ps")
        x1T_done = sem("x1T_done")
        lg_ps = sem("lg_ps")
        rt1 = sem("rt1")
        rt_exp = sem("rt_exp")
        rt2 = sem("rt2")
        RT2 = 15
        cT_ps = sem("cT_ps")
        cT_done = sem("cT_done")
        g_ps = sem("g_ps")
        g_tanh = sem("g_tanh")
        g_read = sem("g_read")
        u_ps = sem("u_ps")
        u_read = sem("u_read")
        cb_ps = sem("cb_ps")
        h_done = sem("h_done")
        dn_ps = sem("dn_ps")
        z2_done = sem("z2_done")
        ln2_stat = sem("ln2_stat")
        ln2_root = sem("ln2_root")
        ln2_inv = sem("ln2_inv")
        out_done = sem("out_done")

        block = ctx.enter_context(nc.Block())

        USES = [
            ("xnT", "P", 1, xnT_done, 2, 2), ("yb3", "F", -1, yb_read, J, 4),
            ("in0", "P", 1, conv_in, 8, 4), ("in1", "P", 1, conv_in, 8, 8),
            ("x1T", "F", -1, x1T_done, 1, 1), ("lg", "F", -1, rt_exp, 2, 2),
            ("yb0", "S", 0, yb_read, J, 1), ("d1", "P", 1, d1_read, 2, 2),
            ("cT", "F", -1, cT_done, 1, 1), ("d2_0", "P", 1, d2_read, 8, 4),
            ("d2_1", "P", 1, d2_read, 8, 8), ("yb1", "S", 0, yb_read, J, 2),
            ("cb0", "F", -1, h_done, FPAIRS, 1), ("cb1", "F", -1, h_done, FPAIRS, 2),
            ("cb2", "F", -1, h_done, FPAIRS, 3), ("cb3", "F", -1, h_done, FPAIRS, 4),
            ("yb2", "S", 0, yb_read, J, 3), ("cb4", "F", -1, h_done, FPAIRS, 5),
            ("cb5", "F", -1, h_done, FPAIRS, 6), ("cb6", "F", -1, h_done, FPAIRS, 7),
            ("skip0", "P", 1, sk_done, 2, 1), ("skip1", "P", 1, sk_done, 2, 2),
        ]
        PLACE = {u[0]: i for i, u in enumerate(USES)}

        def bank(name):
            return work[PLACE[name] % 2]

        def stages(g):
            if g.it is not None:
                return "PSF"
            n = g.base
            return ("P" if n + 1 < NG else "") + ("S" if 0 <= n < NG else "") + ("F" if n >= 1 else "")

        def last_reader(name, g):
            i, body = PLACE[name] - 2, g
            while True:
                if i < 0:
                    i += len(USES)
                    body = body + -1
                    if body.it is None and body.base < -1:
                        return None
                _, stage, off, s, per, k = USES[i]
                if stage in stages(body):
                    return s, (body + off).count(per, k)
                i -= 2

        def run(eng, body):
            body(Group(-1), 1)
            body(Group(0), 0)
            body(Group(1), 1)
            body(Group(2), 0)
            with eng.Fori(0, (NG - 4) // 2) as it:
                body(Group(3, it), 1)
                body(Group(4, it), 0)
            body(Group(NG - 1), 1)
            body(Group(NG), 0)

        @block.sync
        def _(sp):
            for dst, src in ((normw, norm_w), (wxin, w_xin), (convw, conv_w), (convb, conv_b), (idn, ident),
                             (wd1, w_d1), (wd2, w_d2), (bd2, b_d2), (wbc, w_bc), (amat, a_log),
                             (wdd, w_dd), (wout, w_out)):
                sp.dma_start(dst[:], src).then_inc(w_in, 16)
            for dst, src in ((wrt, w_router), (selb, sel), (wg, w_gate), (wu, w_up)):
                sp.dma_start(dst[:], src).then_inc(wf_in, 16)
            sp.dma_start(lower[:], tri).then_inc(wf_in, 16)
            sp.dma_start(wdn[:, 0:FT - 1, :], w_down[0:(FT - 1) * P, :].rearrange("(f p) d -> p f d", p=P))\
                .then_inc(wf_in, 16)
            sp.dma_start(wdn[0:LAST, FT - 1, :], w_down[(FT - 1) * P:FEAT, :]).then_inc(wf_in, 16)

            tokens = resid.rearrange("g (t p) d -> p (g t) d", p=P)
            result = out.rearrange("g (t p) d -> p (g t) d", p=P)

            def body(g, par):
                has, q, f = stages(g), g + 1, g + -1
                rows_q = tokens[:, bass.ds(sp.snap(q.index() * TT), TT), :] if "P" in has else None
                rows_g = tokens[:, bass.ds(sp.snap(g.index() * TT), TT), :] if "S" in has else None
                rows_f = result[:, bass.ds(sp.snap(f.index() * TT), TT), :] if "F" in has else None
                if "P" in has:
                    if g.base >= 0:
                        sp.wait_ge(xn_done, q.count(2, 0))
                    sp.dma_start(xr[:], rows_q).then_inc(xr_in, 16)
                if "S" in has:
                    if g.beyond(2):
                        sp.wait_ge(z2_done, f.count(1, 0))
                    sp.dma_start(x1[:, par], rows_g).then_inc(res_in, 16)
                if "P" in has:
                    stored = q.held(sp, 16, 16)
                    used = [g.held(sp, SLOTS, (J - 1) * NQ + n + 1) for n in range(NQ)]
                    sp.wait_ge(d1_read, q.count(2, 2))
                    sp.dma_start(bcd[1 - par], bcs[:]).then_inc(bc_st, 16)
                    sp.wait_ge(bc_st, stored)
                    for n in range(NQ):
                        if "S" in has:
                            sp.wait_ge(dbx_full, used[n])
                        sp.dma_start(Bb[:, n * QUAD:(n + 1) * QUAD, :],
                                     bcd[1 - par, n * QUAD:(n + 1) * QUAD, :].unsqueeze(0)
                                     .broadcast_to([P, QUAD, L])).then_inc(b_in[n], 16)
                        if "S" in has:
                            sp.wait_ge(cmul_dve, used[n])
                            sp.wait_ge(cmul_pool, used[n])
                        sp.dma_start(Cb[:, n * QUAD:(n + 1) * QUAD, :],
                                     bcd[1 - par, NS + n * QUAD:NS + (n + 1) * QUAD, :].unsqueeze(0)
                                     .broadcast_to([P, QUAD, L])).then_inc(c_in[n], 16)
                if "F" in has:
                    sp.wait_ge(out_done, f.count(2, 2))
                    sp.dma_start(rows_f, ob[:, 1 - par]).then_inc(out_st, 16)

            run(sp, body)
            sp.wait_ge(out_st, 16 * NG)

        @block.tensor
        def _(pe):
            mm = nc.tensor.matmul

            def turn(dst, src, start, stop):
                return mm(dst, src, idn[:], start=start, stop=stop, is_transpose=True, skip_group_check=True)

            def take(name, g):
                w = last_reader(name, g)
                if w is not None:
                    pe.wait_ge(w[0], w[1])

            def body(g, par):
                has, q, f = stages(g), g + 1, g + -1
                qar = 1 - par

                def xnorm_turn():
                    pe.wait_ge(xn_done, q.count(2, 2))
                    take("xnT", g)
                    w = bank("xnT")[:].rearrange("p (k t) -> p k t", k=KD)
                    for k in range(KD):
                        for t in range(TT):
                            last = turn(w[:, k, t * P:(t + 1) * P], xn[:, t, k * P:(k + 1) * P], True, True)
                    last.then_inc(xnT_ps, 1)

                def in_proj(i):
                    if i == 0:
                        pe.wait_ge(xnT_done, q.count(2, 2))
                    take(f"in{i}", g)
                    w = bank(f"in{i}")[:].rearrange("p (h t) -> p h t", h=2)
                    for h in range(2):
                        j = 2 * i + h
                        for k in range(KD):
                            last = mm(w[:, h, :], wxin[:, k, j * P:(j + 1) * P], xnT[:, qar, k, :],
                                      start=(k == 0), stop=(k == KD - 1))
                    last.then_inc(in_ps, 1)

                def skip(i):
                    take(f"skip{i}", g)
                    w = bank(f"skip{i}")[:].rearrange("p (h t) -> p h t", h=2)
                    for h in range(2):
                        j = J + 2 * i + h
                        for k in range(KD):
                            last = mm(w[:, h, :], wxin[:, k, j * P:(j + 1) * P], xnT[:, qar, k, :],
                                      start=(k == 0), stop=(k == KD - 1))
                    last.then_inc(skip_ps, 1)

                def d1():
                    pe.wait_ge(xa_done, q.count(2, 2))
                    take("d1", g)
                    w = bank("d1")
                    for j in range(J):
                        mm(w[:, 0:L], wd1[:, j, :], xa[:, qar, j, :], start=(j == 0), stop=(j == J - 1))
                    for j in range(J):
                        last = mm(w[0:2 * NS, L:2 * L], wbc[:, j, :], xa[:, qar, j, :],
                                  start=(j == 0), stop=(j == J - 1))
                    last.then_inc(d1_ps, 1)

                def d2(i):
                    if i == 0:
                        pe.wait_ge(d1_read, q.count(2, 1))
                    take(f"d2_{i}", g)
                    w = bank(f"d2_{i}")[:].rearrange("p (h t) -> p h t", h=2)
                    for h in range(2):
                        j = 2 * i + h
                        last = mm(w[:, h, :], wd2[:, j * P:(j + 1) * P], r1[:], start=True, stop=True)
                    last.then_inc(d2_ps, 1)

                def y_back(gr, gpar, j):
                    pe.wait_ge(yT_copied, gr.count(J, j + 1))
                    take(f"yb{j}", g)
                    w = bank(f"yb{j}")
                    for t in range(TT):
                        last = turn(w[:, t * P:(t + 1) * P], yTs[:, j % 2, t, :], True, True)
                    last.then_inc(yb_ps, 1)

                def out_proj():
                    pe.wait_ge(yg_done, f.count(J, J))
                    if g.beyond(2):
                        pe.wait_ge(z2_done, f.count(1, 0))
                    for t in range(TT):
                        for j in range(J):
                            last = mm(ops[:, t, :], yg[:, j, t * P:(t + 1) * P], wout[:, j, :],
                                      start=(j == 0), stop=(j == J - 1))
                    last.then_inc(outp_ps, 1)

                def x1_turn():
                    pe.wait_ge(x1_done, f.count(2, 2))
                    take("x1T", g)
                    w = bank("x1T")[:].rearrange("p (k t) -> p k t", k=KD)
                    for k in range(KD):
                        for t in range(TT):
                            last = turn(w[:, k, t * P:(t + 1) * P], x1[:, qar, t, k * P:(k + 1) * P], True, True)
                    last.then_inc(x1T_ps, 1)

                def router():
                    pe.wait_ge(x1T_done, f.count(1, 1))
                    take("lg", g)
                    w = bank("lg")
                    for t in range(TT):
                        for k in range(KD):
                            last = mm(w[:, t * NXS:(t + 1) * NXS], x1T[:, k, t * P:(t + 1) * P], wrt[:, k, :],
                                      start=(k == 0), stop=(k == KD - 1))
                    last.then_inc(lg_ps, 1)

                def comb_turn():
                    pe.wait_ge(rt2, f.count(RT2, RT2))
                    take("cT", g)
                    w = bank("cT")[:].bitcast(BF16)
                    for t in range(TT):
                        last = nc.tensor.transpose(w[0:3 * NXS, t * P:(t + 1) * P],
                                                   cpart[:, t].rearrange("p a b -> p (a b)"), idb[:])
                    last.then_inc(cT_ps, 1)

                def feat_cols(i, h):
                    a = (2 * i + h) * P
                    return a, min(a + P, FEAT)

                def gate(i):
                    pe.wait_ge(x1T_done, f.count(1, 1))
                    if i or g.beyond(2):
                        pe.wait_ge(g_read, f.count(FPAIRS, i))
                    for h in range(2):
                        a, b = feat_cols(i, h)
                        for k in range(KD):
                            last = mm(gps[0:b - a, h, :], wg[:, k, a:b], x1T[:, k, :],
                                      start=(k == 0), stop=(k == KD - 1))
                    last.then_inc(g_ps, 1)

                def up(i):
                    if i or g.beyond(2):
                        pe.wait_ge(u_read, f.count(FPAIRS, i))
                    for h in range(2):
                        a, b = feat_cols(i, h)
                        for k in range(KD):
                            last = mm(ups[0:b - a, h, :], wu[:, k, a:b], x1T[:, k, :],
                                      start=(k == 0), stop=(k == KD - 1))
                    last.then_inc(u_ps, 1)

                def spread(i):
                    if i == 0:
                        pe.wait_ge(cT_done, f.count(1, 1))
                    take(f"cb{i}", g)
                    w = bank(f"cb{i}")[:].rearrange("p (h t) -> p h t", h=2)
                    for h in range(2):
                        a, b = feat_cols(i, h)
                        last = mm(w[0:b - a, h, :], selb[:, a:b], cT[:], start=True, stop=True)
                    last.then_inc(cb_ps, 1)

                def down(i):
                    pe.wait_ge(h_done, f.count(FPAIRS, i + 1))
                    if i == 0:
                        pe.wait_ge(res_sum, f.count(1, 1))
                    for h in range(2):
                        rows = feat_cols(i, h)[1] - feat_cols(i, h)[0]
                        for t in range(TT):
                            first = i == 0 and h == 0
                            last = mm(ops[:, t, :], hh[0:rows, i % HRING, h, t * P:(t + 1) * P], wdn[0:rows, 2 * i + h, :],
                                      start=(first and t == 0), stop=(i == FPAIRS - 1 and h == 1),
                                      skip_group_check=True)
                    last.then_inc(dn_ps, 1)

                def sum_states(gr, c):
                    j, qd = c // NQ, c % NQ
                    if qd == 0 and (j >= 2 or g.beyond(1)):
                        pe.wait_ge(yT_copied, gr.count(J, j - 1))
                    for m in range(2):
                        k = 2 * c + m
                        if m == 0:
                            pe.wait_ge(cmul_dve, gr.count(SLOTS, c + 1))
                        else:
                            pe.wait_ge(cmul_pool, gr.count(SLOTS, c + 1))
                        for n in range(2):
                            for t in range(TT):
                                first = qd == 0 and m == 0 and n == 0
                                last = turn(yT[:, j % 2, t, :], pr[:, k % 4, n, t * P:(t + 1) * P],
                                            first and t == 0, qd == NQ - 1 and m == 1 and n == 1)
                        last.then_inc(summed, 1)

                for s in range(SLOTS):
                    if "P" in has:
                        if s == 1: xnorm_turn()
                    if "F" in has:
                        if s == 1: y_back(f, qar, 3)
                        if s == 2: out_proj()
                    if "P" in has:
                        if s == 2: in_proj(0)
                        if s == 3: in_proj(1)
                    if "F" in has:
                        if s == 4: x1_turn()
                        if s == 5: router(); gate(0)
                    if "S" in has:
                        if s == 5: y_back(g, par, 0)
                    if "F" in has:
                        if s == 6: up(0)
                    if "P" in has:
                        if s == 7: d1()
                    if "F" in has:
                        if s == 7: gate(1)
                        if s == 8: up(1); comb_turn()
                    if "P" in has:
                        if s == 9: d2(0); d2(1)
                    if "F" in has:
                        if s == 9: gate(2)
                    if "S" in has:
                        if s == 9: y_back(g, par, 1)
                    if "F" in has:
                        if s == 10: spread(0); up(2); spread(1)
                        if s == 11: gate(3); spread(2); up(3); down(0)
                        if s == 12: gate(4); spread(3); down(1)
                        if s == 13: up(4); down(2); gate(5)
                    if "S" in has:
                        if s == 13: y_back(g, par, 2)
                    if "F" in has:
                        if s == 14: spread(4); up(5); down(3); gate(6)
                        if s == 15: up(6); spread(5); spread(6); down(4)
                    if "P" in has:
                        if s == 15: skip(0); skip(1)
                    if "F" in has:
                        if s == 15: down(5); down(6)
                    if "S" in has and s >= 1:
                        sum_states(g, s - 1)
                    if "F" in has and s == 0:
                        sum_states(f, SLOTS - 1)

            pe.wait_ge(w_in, 16 * 12)
            pe.wait_ge(wf_in, 16 * 7)
            pe.wait_ge(prep, PREP)
            run(pe, body)

        @block.scalar
        def _(act):
            af = nc.scalar.activation
            act.wait_ge(w_in, 16 * 12)
            af(amat[:], amat[:], ACT.Exp).then_inc(prep_act, 1)
            act.wait_ge(prep, PREP)

            def body(g, par):
                has, q, f = stages(g), g + 1, g + -1
                qar = 1 - par

                def mean_square():
                    act.wait_ge(xr_in, q.count(16, 16))
                    for t in range(TT):
                        if t or g.base >= 0:
                            act.wait_ge(squares, q.count(2, t))
                        af(sqd[:], xr[:, t, :], ACT.Square, accum_out=ss[:, t:t + 1]).then_inc(squares, 1)
                    act.wait_ge(squares, q.count(2, 2))
                    af(rms[:], ss[:], ACT.Sqrt, bias=eps[:], scale=1.0 / D).then_inc(rms_root, 1)

                def normalise():
                    act.wait_ge(rms_inv, q.count(1, 1))
                    if g.base >= 0:
                        act.wait_ge(xnT_ps, q.count(1, 0))
                    for t in range(TT):
                        af(xn[:, t, :], xr[:, t, :], ACT.Copy, scale=rinv[:, t:t + 1]).then_inc(xn_done, 1)

                def copy_xnT():
                    act.wait_ge(xnT_ps, q.count(1, 1))
                    w = bank("xnT")[:].rearrange("p (k t) -> p k t", k=KD)
                    for k in range(KD):
                        af(xnT[:, qar, k, :], w[:, k, :], ACT.Copy, scale=normw[:, k:k + 1]).then_inc(xnT_done, 1)

                def conv_first(i):
                    act.wait_ge(in_ps, q.count(2, i + 1))
                    if i == 0 and g.base >= 0:
                        act.wait_ge(xa_done, q.count(2, 0))
                    w = bank(f"in{i}")[:].rearrange("p (h t) -> p h t", h=2)
                    for h in range(2):
                        j = 2 * i + h
                        af(xin[:, j, TAPS - 1:], w[:, h, :], ACT.Copy).then_inc(conv_in, 1)
                        af(cv[:, j, :], w[:, h, :], ACT.Identity, bias=convb[:, j:j + 1],
                           scale=convw[:, j, TAPS - 1:TAPS]).then_inc(conv_in, 1)

                def conv_sig(i):
                    act.wait_ge(conv_step, q.count(12, 6 * i + 6))
                    af(xa[:, qar, 2 * i:2 * i + 2, :], cv[:, 2 * i:2 * i + 2, :], ACT.Tanh).then_inc(conv_tanh, 1)

                def copy_d1():
                    act.wait_ge(d1_ps, q.count(1, 1))
                    if g.base >= 0:
                        act.wait_ge(bc_st, q.count(16, 0))
                    w = bank("d1")
                    af(r1[:], w[:, 0:L], ACT.Copy).then_inc(d1_read, 1)
                    af(bcs[:], w[0:2 * NS, L:2 * L], ACT.Copy).then_inc(d1_read, 1)

                def softplus_parts(i):
                    act.wait_ge(d2_ps, q.count(2, i + 1))
                    if i == 0 and g.base >= 0:
                        act.wait_ge(sp_pool, q.count(3, 0))
                    w = bank(f"d2_{i}")[:].rearrange("p (h t) -> p h t", h=2)
                    for h in range(2):
                        j = 2 * i + h
                        af(spz[:, j, :], w[:, h, :], ACT.Abs, bias=bd2[:, j:j + 1]).then_inc(d2_read, 1)
                        af(spr[:, j, :], w[:, h, :], ACT.Relu, bias=bd2[:, j:j + 1]).then_inc(d2_read, 1)

                def softplus_exp():
                    act.wait_ge(d2_read, q.count(8, 8))
                    af(spz[:], spz[:], ACT.Exp, scale=-1.0).then_inc(sp_exp, 1)

                def softplus_log():
                    act.wait_ge(sp_exp, q.count(1, 1))
                    af(dlt[:, qar], spz[:], ACT.Ln, bias=1.0).then_inc(sp_ln, 1)

                def skip_sig(i):
                    act.wait_ge(skip_ps, q.count(2, i + 1))
                    if "F" in has:
                        act.wait_ge(yg_done, f.count(J, J))
                    af(sk[:, qar, 2 * i:2 * i + 2, :], bank(f"skip{i}")[:].rearrange("p (h t) -> p h t", h=2), ACT.Tanh,
                       scale=0.5).then_inc(skip_tanh, 1)

                def copy_yT(gr, j):
                    act.wait_ge(summed, gr.count(PAIRS, PJ * (j + 1)))
                    if j >= 2 or gr.beyond(1):
                        act.wait_ge(yb_ps, gr.count(J, j - 1))
                    af(yTs[:, j % 2], yT[:, j % 2], ACT.Copy).then_inc(yT_copied, 1)

                def decay(c):
                    j = c // NQ
                    if c == 0:
                        act.wait_ge(dlt_done, g.count(1, 1))
                    for m in range(2):
                        k = 2 * c + m
                        if k >= 2 or g.beyond(1):
                            if m == 0:
                                act.wait_ge(cmul_dve, g.count(SLOTS, c))
                            else:
                                act.wait_ge(scan_done, g.count(PAIRS, k - 1))
                        for n in range(2):
                            ns = 2 * (k % PJ) + n
                            lo = m
                            ins = af(dA[m][:, n, lo:], dlt[:, par, j, lo:], ACT.Exp,
                                     scale=amat[:, j, ns:ns + 1])
                        ins.then_inc(dA_full, 1)

                def root1():
                    act.wait_ge(ln1_stat, f.count(4, 4))
                    af(sd1[:], mv1[:, :, 1], ACT.Sqrt, bias=eps[:]).then_inc(ln1_root, 1)

                def root2():
                    act.wait_ge(ln2_stat, f.count(4, 4))
                    af(sd2[:], mv2[:, :, 1], ACT.Sqrt, bias=eps[:]).then_inc(ln2_root, 1)

                def copy_x1T():
                    act.wait_ge(x1T_ps, f.count(1, 1))
                    af(x1T[:].rearrange("p k t -> p (k t)"), bank("x1T")[:], ACT.Copy).then_inc(x1T_done, 1)

                def route_exp():
                    act.wait_ge(rt1, f.count(2, 2))
                    af(ex[:], ex[:], ACT.Exp).then_inc(rt_exp, 1)
                    w = bank("lg")[:, 0:TT * NXS].rearrange("p (t x) -> p t x", t=TT)
                    af(sgt[:], w[:, :, NX:NXS], ACT.Tanh, scale=0.5).then_inc(rt_exp, 1)

                def copy_cT():
                    act.wait_ge(cT_ps, f.count(1, 1))
                    af(cT[:], bank("cT")[:].bitcast(BF16)[0:3 * NXS, 0:L], ACT.Copy).then_inc(cT_done, 1)

                def gate_sig(i):
                    act.wait_ge(g_ps, f.count(FPAIRS, i + 1))
                    if i >= HRING or g.beyond(2):
                        act.wait_ge(dn_ps, f.count(FPAIRS, max(i - HRING + 1, 0)))
                    af(hh[:, i % HRING], gps[:], ACT.Tanh, scale=0.5).then_inc(g_tanh, 1)

                for s in range(SLOTS):
                    if "P" in has:
                        if s == 0: mean_square()
                        if s == 1: normalise()
                    if "F" in has:
                        if s == 1: copy_yT(f, 3)
                    if "P" in has:
                        if s == 2: copy_xnT()
                        if s == 3: conv_first(0)
                    if "F" in has:
                        if s == 3: root1()
                    if "P" in has:
                        if s == 4: conv_first(1)
                        if s == 5: conv_sig(0)
                    if "F" in has:
                        if s == 5: copy_x1T()
                    if "S" in has:
                        if s == 5: copy_yT(g, 0)
                    if "P" in has:
                        if s == 6: conv_sig(1)
                    if "F" in has:
                        if s == 6: gate_sig(0); route_exp()
                    if "P" in has:
                        if s == 8: copy_d1()
                    if "F" in has:
                        if s == 8: gate_sig(1)
                        if s == 9: copy_cT()
                    if "P" in has:
                        if s == 9: softplus_parts(0); softplus_parts(1)
                    if "S" in has:
                        if s == 9: copy_yT(g, 1)
                    if "P" in has:
                        if s == 10: softplus_exp()
                    if "F" in has:
                        if s == 10: gate_sig(2)
                    if "P" in has:
                        if s == 11: softplus_log()
                    if "F" in has:
                        if s == 12: gate_sig(3)
                        if s == 13: gate_sig(4)
                    if "S" in has:
                        if s == 13: copy_yT(g, 2)
                    if "F" in has:
                        if s == 14: gate_sig(5)
                        if s == 15: gate_sig(6)
                    if "P" in has:
                        if s == 15: skip_sig(0); skip_sig(1)
                    if "S" in has:
                        decay(s)
                    if "F" in has:
                        if s == 15: root2()

            run(act, body)

        @block.gpsimd
        def _(pool):
            def body(g, par):
                has, q, f = stages(g), g + 1, g + -1

                def softplus_rest():
                    if g.base >= 0:
                        pool.wait_ge(dlt_done, q.count(1, 0))
                    need = q.held(pool, 1, 1)
                    pool.wait_ge(prep, PREP)
                    pool.wait_ge(sp_exp, need)
                    nc.gpsimd.tensor_scalar(spu[:], spz[:], 1.0, -1.0, ALU.add, ALU.add).then_inc(sp_pool, 1)
                    pool.wait_ge(sp_pool, q.count(3, 1))
                    nc.gpsimd.tensor_tensor(spu[:], spz[:], spu[:], ALU.subtract).then_inc(sp_pool, 1)
                    pool.wait_ge(sp_pool, q.count(3, 2))
                    nc.gpsimd.tensor_tensor(spu[:], spr[:], spu[:], ALU.add).then_inc(sp_pool, 1)

                def drive(c):
                    j, qd = c // NQ, c % NQ
                    if c == 0:
                        pool.wait_ge(dx_done, g.count(1, 1))
                    if j == 0:
                        pool.wait_ge(b_in[qd], g.count(16, 16))
                    if c >= 2 or g.beyond(1):
                        pool.wait_ge(scan_done, g.count(PAIRS, 2 * (c - 1)))
                    nc.gpsimd.tensor_tensor(
                        dbx[:, c % 2], dx[:, par, j, :].unsqueeze(1).broadcast_to([P, QUAD, L]),
                        Bb[:, qd * QUAD:(qd + 1) * QUAD, :], ALU.mult).then_inc(dbx_full, 1)

                def weigh(gr, c):
                    k, qd = 2 * c + 1, c % NQ
                    pool.wait_ge(scan_done, gr.count(PAIRS, k + 1))
                    if c < NQ:
                        pool.wait_ge(c_in[qd], gr.count(16, 16))
                    nc.gpsimd.tensor_tensor(pr[:, k % 4], pr[:, k % 4],
                                            Cb[:, qd * QUAD + 2:(qd + 1) * QUAD, :], ALU.mult)\
                        .then_inc(cmul_pool, 1)

                for s in range(SLOTS):
                    if "P" in has and s == 11:
                        softplus_rest()
                    if "S" in has:
                        drive(s)
                        if s >= 1:
                            weigh(g, s - 1)
                        if s == SLOTS - 1:
                            weigh(g, s)

            run(pool, body)

        @block.vector
        def _(dve):
            ts, tt, stt = nc.vector.tensor_scalar, nc.vector.tensor_tensor, nc.vector.scalar_tensor_tensor
            nc.vector.memset(xin[:, :, 0:TAPS - 1], 0.0).then_inc(prep, 1)
            nc.vector.memset(dA[1][:, :, 0:1], 0.0).then_inc(prep, 1)
            nc.vector.memset(eps[:], EPS).then_inc(prep, 1)
            dve.wait_ge(w_in, 16 * 12)
            ts(convw[:], convw[:], 0.5, None, ALU.mult).then_inc(prep, 1)
            ts(convb[:], convb[:], 0.5, None, ALU.mult).then_inc(prep, 1)
            ts(wout[:], wout[:], 0.5, None, ALU.mult).then_inc(prep, 1)
            nc.vector.tensor_copy(idb[:], idn[:]).then_inc(prep, 1)
            dve.wait_ge(prep_act, 1)
            ts(amat[:], amat[:], -1.0, None, ALU.mult).then_inc(prep_act, 1)

            def body(g, par):
                has, q, f = stages(g), g + 1, g + -1
                qar = 1 - par

                def rms_recip():
                    dve.wait_ge(rms_root, q.count(1, 1))
                    nc.vector.reciprocal(rinv[:], rms[:]).then_inc(rms_inv, 1)

                def conv(i):
                    for tap in range(TAPS - 1):
                        for h in range(2):
                            j = 2 * i + h
                            n = 6 * i + 2 * tap + h
                            if tap == 0:
                                dve.wait_ge(conv_in, q.count(8, 2 * j + 2))
                            else:
                                dve.wait_ge(conv_step, q.count(12, n - 1))
                            stt(cv[:, j, :], xin[:, j, tap:tap + L], convw[:, j, tap:tap + 1], cv[:, j, :],
                                ALU.mult, ALU.add).then_inc(conv_step, 1)

                def conv_silu(i):
                    dve.wait_ge(conv_tanh, q.count(2, i + 1))
                    stt(xa[:, qar, 2 * i:2 * i + 2, :], xa[:, qar, 2 * i:2 * i + 2, :], 1.0, cv[:, 2 * i:2 * i + 2, :],
                        ALU.add, ALU.mult).then_inc(xa_done, 1)

                def delta():
                    dve.wait_ge(sp_ln, q.count(1, 1))
                    dve.wait_ge(sp_pool, q.count(3, 3))
                    tt(dlt[:, qar], dlt[:, qar], spu[:], ALU.add).then_inc(dlt_done, 1)
                    dve.wait_ge(dlt_done, q.count(1, 1))
                    tt(dx[:, qar], dlt[:, qar], xa[:, qar], ALU.mult).then_inc(dx_done, 1)

                def skip_silu(i):
                    dve.wait_ge(skip_tanh, q.count(2, i + 1))
                    stt(sk[:, qar, 2 * i:2 * i + 2, :], sk[:, qar, 2 * i:2 * i + 2, :], 1.0,
                        bank(f"skip{i}")[:].rearrange("p (h t) -> p h t", h=2),
                        ALU.add, ALU.mult).then_inc(sk_done, 1)

                def y_gate(gr, gpar, j):
                    dve.wait_ge(yb_ps, gr.count(J, j + 1))
                    stt(yd[:, j % 2, :], xa[:, gpar, j, :], wdd[:, j:j + 1], bank(f"yb{j}")[:, 0:L],
                        ALU.mult, ALU.add).then_inc(yb_read, 1)
                    dve.wait_ge(yb_read, gr.count(J, j + 1))
                    if j == 0 and gr.beyond(1):
                        dve.wait_ge(outp_ps, gr.count(1, 0))
                    tt(yg[:, j, :], yd[:, j % 2, :], sk[:, gpar, j, :], ALU.mult).then_inc(yg_done, 1)

                def res_norm_stats():
                    dve.wait_ge(outp_ps, f.count(1, 1))
                    dve.wait_ge(res_in, f.count(16, 16))
                    stt(x1[:, qar], x1[:, qar], 2.0, ops[:], ALU.mult, ALU.add).then_inc(res_sum, 1)
                    dve.wait_ge(res_sum, f.count(1, 1))
                    for t in range(TT):
                        nc.vector.bn_stats(st1[:, t, :], x1[:, qar, t, :]).then_inc(ln1_stat, 1)
                    for t in range(TT):
                        need = f.held(dve, 4, t + 1)
                        dve.wait_ge(prep, PREP)
                        dve.wait_ge(ln1_stat, need)
                        nc.vector.bn_aggr(mv1[:, t, :], st1[:, t, :]).then_inc(ln1_stat, 1)

                def res_norm():
                    dve.wait_ge(ln1_root, f.count(1, 1))
                    nc.vector.reciprocal(ri1[:], sd1[:]).then_inc(ln1_inv, 1)
                    dve.wait_ge(ln1_inv, f.count(1, 1))
                    for t in range(TT):
                        ts(x1[:, qar, t, :], x1[:, qar, t, :], mv1[:, t, 0:1], ri1[:, t:t + 1],
                           ALU.subtract, ALU.mult).then_inc(x1_done, 1)

                def route_max():
                    dve.wait_ge(lg_ps, f.count(1, 1))
                    lg = bank("lg")[:, 0:TT * NXS].rearrange("p (t x) -> p t x", t=TT)[:, :, 0:NX]
                    nc.vector.tensor_reduce(lmax[:], lg, AX.X, ALU.max).then_inc(rt1, 1)
                    dve.wait_ge(rt1, f.count(2, 1))
                    tt(ex[:], lg, lmax[:].unsqueeze(2).broadcast_to([P, TT, NX]), ALU.subtract).then_inc(rt1, 1)

                def route_top2():
                    step = [0]

                    def then(ins):
                        step[0] += 1
                        ins.then_inc(rt2, 1)

                    def settle():
                        dve.wait_ge(rt2, f.count(RT2, step[0]))

                    other = ex[:].unsqueeze(2).broadcast_to([P, TT, NX, NX])
                    own = ex[:].unsqueeze(3).broadcast_to([P, TT, NX, NX])
                    dve.wait_ge(rt_exp, f.count(2, 2))
                    then(tt(gt[:], other, own, ALU.is_gt))
                    then(tt(eq[:], other, own, ALU.is_equal))
                    settle()
                    then(tt(eq[:], eq[:], lower[:].unsqueeze(1).broadcast_to([P, TT, NX, NX]), ALU.mult))
                    settle()
                    then(tt(gt[:], gt[:], eq[:], ALU.add))
                    settle()
                    then(nc.vector.tensor_reduce(rank[:], gt[:], AX.X, ALU.add))
                    settle()
                    then(stt(top[:], rank[:], 2.0, ex[:], ALU.is_lt, ALU.mult))
                    settle()
                    then(nc.vector.tensor_reduce(tsum[:], top[:], AX.X, ALU.add))
                    settle()
                    then(nc.vector.reciprocal(tinv[:], tsum[:]))
                    settle()
                    then(stt(comb[:, :, 0:NX], top[:], 0.5, tinv[:].unsqueeze(2).broadcast_to([P, TT, NX]),
                             ALU.mult, ALU.mult))
                    then(ts(comb[:, :, NX:NXS], sgt[:], 0.25, 0.25, ALU.mult, ALU.add))
                    settle()
                    then(nc.vector.tensor_copy(cpart[:, :, 0, :], comb[:]))
                    settle()
                    then(tt(crest[:], comb[:], cpart[:, :, 0, :], ALU.subtract))
                    settle()
                    then(nc.vector.tensor_copy(cpart[:, :, 1, :], crest[:]))
                    settle()
                    then(tt(comb[:], crest[:], cpart[:, :, 1, :], ALU.subtract))
                    settle()
                    then(nc.vector.tensor_copy(cpart[:, :, 2, :], comb[:]))
                    assert step[0] == RT2

                def glu_gate(i):
                    dve.wait_ge(g_tanh, f.count(FPAIRS, i + 1))
                    stt(hh[:, i % HRING], hh[:, i % HRING], 1.0, gps[:], ALU.add, ALU.mult).then_inc(g_read, 1)

                def glu_up(i):
                    dve.wait_ge(g_read, f.count(FPAIRS, i + 1))
                    dve.wait_ge(u_ps, f.count(FPAIRS, i + 1))
                    tt(hh[:, i % HRING], hh[:, i % HRING], ups[:], ALU.mult).then_inc(u_read, 1)

                def glu_weigh(i):
                    dve.wait_ge(u_read, f.count(FPAIRS, i + 1))
                    dve.wait_ge(cb_ps, f.count(FPAIRS, i + 1))
                    tt(hh[:, i % HRING], hh[:, i % HRING], bank(f"cb{i}")[:].rearrange("p (h t) -> p h t", h=2),
                       ALU.mult).then_inc(h_done, 1)

                def out_norm():
                    dve.wait_ge(dn_ps, f.count(FPAIRS, FPAIRS))
                    if g.beyond(3):
                        dve.wait_ge(out_st, f.count(16, -16))
                    tt(ob[:, qar], x1[:, qar], ops[:], ALU.add).then_inc(z2_done, 1)
                    dve.wait_ge(z2_done, f.count(1, 1))
                    for t in range(TT):
                        nc.vector.bn_stats(st2[:, t, :], ob[:, qar, t, :]).then_inc(ln2_stat, 1)
                    for t in range(TT):
                        need = f.held(dve, 4, t + 1)
                        dve.wait_ge(prep, PREP)
                        dve.wait_ge(ln2_stat, need)
                        nc.vector.bn_aggr(mv2[:, t, :], st2[:, t, :]).then_inc(ln2_stat, 1)
                    dve.wait_ge(ln2_root, f.count(1, 1))
                    nc.vector.reciprocal(ri2[:], sd2[:]).then_inc(ln2_inv, 1)
                    dve.wait_ge(ln2_inv, f.count(1, 1))
                    for t in range(TT):
                        ts(ob[:, qar, t, :], ob[:, qar, t, :], mv2[:, t, 0:1], ri2[:, t:t + 1],
                           ALU.subtract, ALU.mult).then_inc(out_done, 1)

                def scan(c):
                    j, qd = c // NQ, c % NQ
                    k = 2 * c
                    mul, add = ALU.mult, ALU.add
                    dve.wait_ge(dbx_full, g.count(SLOTS, c + 1))
                    dve.wait_ge(dA_full, g.count(PAIRS, k + 1))
                    for n in range(2):
                        ins = nc.vector.tensor_tensor_scan(dA[0][:, n, :], dA[0][:, n, :], dbx[:, c % 2, n, :],
                                                           0.0, mul, add)
                    ins.then_inc(scan_done, 1)
                    dve.wait_ge(dA_full, g.count(PAIRS, k + 2))
                    if c >= 2 or g.beyond(1):
                        dve.wait_ge(summed, g.count(PAIRS, k - 2))
                    nc.vector.tensor_tensor_scan(
                        pr[:, (k + 1) % 4].rearrange("p n t -> p (n t)"), dA[1][:].rearrange("p n t -> p (n t)"),
                        dbx[:, c % 2, 2:4, :].rearrange("p n t -> p (n t)"), 0.0, mul, add).then_inc(scan_done, 1)
                    dve.wait_ge(scan_done, g.count(PAIRS, k + 1))
                    if j == 0:
                        dve.wait_ge(c_in[qd], g.count(16, 16))
                    tt(pr[:, k % 4], dA[0][:], Cb[:, qd * QUAD:qd * QUAD + 2, :], mul).then_inc(cmul_dve, 1)

                for s in range(SLOTS):
                    if "P" in has:
                        if s == 0: rms_recip()
                    if "F" in has:
                        if s == 2: y_gate(f, qar, 3)
                        if s == 3: res_norm_stats()
                        if s == 4: res_norm()
                    if "P" in has:
                        if s == 4: conv(0)
                        if s == 5: conv(1)
                        if s == 6: conv_silu(0); conv_silu(1)
                    if "F" in has:
                        if s == 6: route_max()
                    if "S" in has:
                        if s == 6: y_gate(g, par, 0)
                    if "F" in has:
                        if s == 7: glu_gate(0); route_top2()
                        if s == 8: glu_up(0)
                        if s == 9: glu_gate(1); glu_up(1)
                        if s == 10: glu_gate(2)
                    if "S" in has:
                        if s == 10: y_gate(g, par, 1)
                    if "F" in has:
                        if s == 11: glu_weigh(0); glu_up(2); glu_weigh(1)
                        if s == 12: glu_gate(3); glu_weigh(2); glu_up(3)
                        if s == 13: glu_gate(4); glu_weigh(3)
                    if "P" in has:
                        if s == 13: delta()
                    if "F" in has:
                        if s == 14: glu_up(4); glu_gate(5)
                    if "S" in has:
                        if s == 14: y_gate(g, par, 2)
                    if "F" in has:
                        if s == 15: glu_weigh(4); glu_up(5); glu_gate(6); glu_weigh(5); glu_up(6); glu_weigh(6)
                    if "P" in has:
                        if s == 15: skip_silu(0); skip_silu(1)
                    if "S" in has:
                        scan(s)
                    if "F" in has:
                        if s == 15: out_norm()

            run(dve, body)


_OUT = (16, 256, 256)


def kernel(**inputs):
    import ml_dtypes
    import numpy as np
    import concourse.bacc as _bacc
    from concourse import mybir as _mybir
    from concourse.bass_utils import run_bass_kernel_spmd as _run

    a = {k: np.asarray(v) for k, v in inputs.items()}
    P = 128

    def rows(w):
        n = w.shape[0] // P
        return np.ascontiguousarray(w.reshape(n, P, -1).swapaxes(0, 1))

    attn = lambda n: a["L0_attn_" + n]
    ffn = lambda n: a["L0_ffn_" + n]
    NX, D, H = ffn("w_gate").shape
    HS = ffn("shw_gate").shape[1]
    FEAT = NX * H + HS
    owner = np.concatenate([np.repeat(np.arange(NX), H), np.full(HS, NX)])
    sel = (owner[None, :] == (np.arange(3 * (NX + 1)) % (NX + 1))[:, None]).astype(np.float32)
    tri = np.ascontiguousarray(np.broadcast_to(np.tril(np.ones((NX, NX), np.float32), -1), (P, NX, NX)))
    side = lambda w, sh: np.concatenate([w.transpose(1, 0, 2).reshape(D, NX * H), sh], axis=1)
    arrays = {
        "resid": attn("resid"),
        "w_xin": rows(np.concatenate([attn("W_in"), attn("W_skip")], axis=0).T),
        "norm_w": rows(attn("norm_w"))[:, :, 0],
        "conv_w": rows(attn("conv_w")),
        "conv_b": rows(attn("conv_b"))[:, :, 0],
        "w_d1": rows(attn("W_d1").T),
        "w_d2": attn("W_d2").T,
        "b_d2": rows(attn("b_d2"))[:, :, 0],
        "w_bc": rows(np.concatenate([attn("W_Bm"), attn("W_Cm")], axis=0).T),
        "a_log": rows(attn("A_log")),
        "w_dd": rows(attn("W_D"))[:, :, 0],
        "w_out": rows(attn("W_out").T),
        "w_router": rows(np.concatenate([ffn("gate_w"), ffn("shgate_w")[None, :]], axis=0).T),
        "w_gate": rows(side(ffn("w_gate"), ffn("shw_gate"))),
        "w_up": rows(side(ffn("w_up"), ffn("shw_up"))),
        "w_down": np.concatenate([ffn("w_down").reshape(NX * H, D), ffn("shw_down")], axis=0),
        "sel": sel.astype(ml_dtypes.bfloat16),
        "tri": tri,
        "ident": np.eye(P, dtype=np.float32),
    }
    arrays = {f"{k}_dram": np.ascontiguousarray(v) for k, v in arrays.items()}
    nc = _bacc.Bacc("TRN2", target_bir_lowering=False, num_devices=1)
    args = [nc.dram_tensor(k, v.shape, _mybir.dt.from_np(v.dtype), kind="ExternalInput").ap()
            for k, v in arrays.items()]
    args.append(nc.dram_tensor("out_dram", _OUT, _mybir.dt.float32, kind="ExternalOutput").ap())
    build(nc, *args)
    r = _run(nc, [arrays], core_ids=[0])
    return r.results[0]["out_dram"]
```

```python
from contextlib import ExitStack

import concourse.bass as bass
from concourse import mybir

ALU = mybir.AluOpType
ACT = mybir.ActivationFunctionType
AX = mybir.AxisListType
F32 = mybir.dt.float32
BF16 = mybir.dt.bfloat16

P = 128
EPS = 1e-5


class Group:

    def __init__(self, base, it=None):
        self.base, self.it = base, it

    def __add__(self, d):
        return Group(self.base + d, self.it)

    def count(self, per, k):
        fixed = self.base * per + k
        return fixed if self.it is None else self.it * (2 * per) + fixed

    def held(self, eng, per, k):
        if self.it is None:
            return self.count(per, k)
        reg = eng.alloc_register()
        eng.reg_mov(reg, self.count(per, k))
        return eng.snap(reg)

    def beyond(self, n):
        return self.base >= n

    def index(self):
        return self.base if self.it is None else self.it * 2 + self.base


def build(nc, resid, w_xin, norm_w, conv_w, conv_b, w_d1, w_d2, b_d2, w_bc, a_log, w_dd, w_out,
          w_router, w_gate, w_up, w_down, sel, tri, ident, out):
    NG, L, D = resid.shape
    TT = L // P
    KD = D // P
    E = w_dd.shape[0] * w_dd.shape[1]
    J = E // P
    NS = a_log.shape[2]
    R = w_d2.shape[0]
    TAPS = conv_w.shape[2]
    NX = w_router.shape[2] - 1
    NXS = NX + 1
    FEAT = w_gate.shape[2]
    FT = (FEAT + P - 1) // P
    FPAIRS = FT // 2
    LAST = FEAT - (FT - 1) * P
    QUAD = 4
    NQ = NS // QUAD
    SLOTS = J * NQ
    PAIRS = 2 * SLOTS
    DRING = 4
    HRING = 4
    PJ = NS // 2
    assert TT == 2 and KD == 2 and J == 4 and FT == 14 and TAPS == 4 and R == P and NX == 8

    with ExitStack() as ctx:
        def sb(name, shape, dt=F32):
            return ctx.enter_context(nc.sbuf_tensor(name, shape, dt))

        def ps(name, shape, dt=F32):
            return ctx.enter_context(nc.psum_tensor(name, shape, dt))

        def sem(name):
            return ctx.enter_context(nc.semaphore(name))

        wxin = sb("wxin", [P, KD, 2 * E])
        normw = sb("normw", [P, KD])
        convw = sb("convw", [P, J, TAPS])
        convb = sb("convb", [P, J])
        wd1 = sb("wd1", [P, J, R])
        wd2 = sb("wd2", [R, E])
        bd2 = sb("bd2", [P, J])
        wbc = sb("wbc", [P, J, 2 * NS])
        amat = sb("amat", [P, J, NS])
        wdd = sb("wdd", [P, J])
        wout = sb("wout", [P, J, D])
        wrt = sb("wrt", [P, KD, NXS])
        wg = sb("wg", [P, KD, FEAT])
        wu = sb("wu", [P, KD, FEAT])
        wdn = sb("wdn", [P, FT, D])
        selb = sb("selb", [3 * NXS, FEAT], BF16)
        lower = sb("lower", [P, NX, NX])
        idn = sb("idn", [P, P])
        idb = sb("idb", [P, P], BF16)
        eps = sb("eps", [P, 1])

        xr = sb("xr", [P, TT, D])
        sqd = sb("sqd", [P, D])
        mv = sb("mv", [P, 3, TT, 2])
        root = sb("root", [P, 3, TT])
        inv = sb("inv", [P, 3, TT])
        xn = sb("xn", [P, TT, D])
        xnT = sb("xnT", [P, 2, KD, L])
        xin = sb("xin", [P, J, TAPS - 1 + L])
        xa = sb("xa", [P, 2, J, L])
        r1 = sb("r1", [P, L])
        bcs = sb("bcs", [2 * NS, L])
        spz = sb("spz", [P, J, L])
        spu = sb("spu", [P, J, L])
        dlt = sb("dlt", [P, 2, J, L])
        dx = sb("dx", [P, 2, J, L])
        sk = sb("sk", [P, 2, J, L])

        Bb = sb("Bb", [P, NS, L])
        Cb = sb("Cb", [P, NS, L])
        dbx = sb("dbx", [P, DRING, QUAD, L])
        pr = sb("pr", [P, 4, 2, L])
        yTs = sb("yTs", [P, 2, TT, P])
        yd = sb("yd", [P, 2, L])
        yg = sb("yg", [P, J, L])

        x1 = sb("x1", [P, 2, TT, D])
        st1 = sb("st1", [P, TT, 6])
        st2 = sb("st2", [P, TT, 6])
        x1T = sb("x1T", [P, KD, L])
        lmax = sb("lmax", [P, TT])
        ex = sb("ex", [P, TT, NX])
        sgt = sb("sgt", [P, TT, 1])
        gt = sb("gt", [P, TT, NX, NX])
        eq = sb("eq", [P, TT, NX, NX])
        rank = sb("rank", [P, TT, NX])
        top = sb("top", [P, TT, NX])
        tsum = sb("tsum", [P, TT])
        tinv = sb("tinv", [P, TT])
        comb = sb("comb", [P, TT, NXS])
        cpart = sb("cpart", [P, TT, 3, NXS], BF16)
        crest = sb("crest", [P, TT, NXS])
        cT = sb("cT", [3 * NXS, L], BF16)
        hh = sb("hh", [P, HRING, 2, L])
        ob = sb("ob", [P, TT, D])

        bcd = nc.dram_tensor("bc_scratch", [2, 2 * NS, L], F32, kind="Internal").ap()

        dA = [ps(f"dA{i}", [P, 2, L]) for i in range(2)]
        yT = ps("yT", [P, 2, TT, P])
        work = [ps(f"work{i}", [P, 512]) for i in range(2)]
        gps = ps("gps", [P, 2, L])
        ups = ps("ups", [P, 2, L])
        ops = ps("ops", [P, TT, D])

        w0_in = sem("w0_in")
        w_in = sem("w_in")
        wf_in = sem("wf_in")
        prep_act = sem("prep_act")
        prep = sem("prep")
        prep_wout = sem("prep_wout")
        PREP = 6
        xr_in = sem("xr_in")
        res_in = sem("res_in")
        bc_st = sem("bc_st")
        b_in = [sem(f"b_in{q}") for q in range(NQ)]
        c_in = [sem(f"c_in{q}") for q in range(NQ)]
        out_st = sem("out_st")
        squares = sem("squares")
        roots = sem("roots")
        inverses = sem("inverses")
        xn_done = sem("xn_done")
        xnT_ps = sem("xnT_ps")
        xnT_done = sem("xnT_done")
        in_ps = sem("in_ps")
        conv_in = sem("conv_in")
        conv_step = sem("conv_step")
        conv_tanh = sem("conv_tanh")
        xa_done = sem("xa_done")
        d1_ps = sem("d1_ps")
        d1_read = sem("d1_read")
        d2_ps = sem("d2_ps")
        d2_read = sem("d2_read")
        sp_exp = sem("sp_exp")
        sp_ln = sem("sp_ln")
        sp_low = sem("sp_low")
        sp_pool = sem("sp_pool")
        dlt_done = sem("dlt_done")
        dx_done = sem("dx_done")
        skip_ps = sem("skip_ps")
        skip_tanh = sem("skip_tanh")
        sk_done = sem("sk_done")
        dA_full = sem("dA_full")
        dbx_full = sem("dbx_full")
        scan_done = sem("scan_done")
        cmul_dve = sem("cmul_dve")
        cmul_pool = sem("cmul_pool")
        summed = sem("summed")
        yT_copied = sem("yT_copied")
        yb_ps = sem("yb_ps")
        yb_read = sem("yb_read")
        yg_done = sem("yg_done")
        outp_ps = sem("outp_ps")
        res_sum = sem("res_sum")
        ln1_stat = sem("ln1_stat")
        x1_done = sem("x1_done")
        x1T_ps = sem("x1T_ps")
        x1T_done = sem("x1T_done")
        lg_ps = sem("lg_ps")
        rt1 = sem("rt1")
        rt_exp = sem("rt_exp")
        rt2 = sem("rt2")
        RT2 = 15
        cT_ps = sem("cT_ps")
        cT_done = sem("cT_done")
        g_ps = sem("g_ps")
        g_tanh = sem("g_tanh")
        g_read = sem("g_read")
        u_ps = sem("u_ps")
        u_read = sem("u_read")
        cb_ps = sem("cb_ps")
        h_done = sem("h_done")
        dn_ps = sem("dn_ps")
        z2_done = sem("z2_done")
        ln2_stat = sem("ln2_stat")
        ln2_root = sem("ln2_root")
        ln2_inv = sem("ln2_inv")
        out_done = sem("out_done")

        block = ctx.enter_context(nc.Block())

        USES = [
            ("skip0", 1, "S", 0, sk_done, 2, 1),
            ("cb5", 0, "T", -2, h_done, FPAIRS, 6),
            ("skip1", 0, "S", 0, sk_done, 2, 2),
            ("yb3", 0, "F", -1, yb_read, J, 4),
            ("outp", 0, "F", -1, res_sum, 1, 1),
            ("cb6", 1, "T", -2, h_done, FPAIRS, 7),
            ("xnT", 0, "P", 1, xnT_done, 2, 2),
            ("x1T", 1, "F", -1, x1T_done, 1, 1),
            ("lg", 0, "F", -1, rt_exp, 2, 2),
            ("in0", 1, "P", 1, conv_in, 8, 4),
            ("in1", 0, "P", 1, conv_in, 8, 8),
            ("yb0", 0, "S", 0, yb_read, J, 1),
            ("cT", 1, "F", -1, cT_done, 1, 1),
            ("cb0", 0, "F", -1, h_done, FPAIRS, 1),
            ("d1", 1, "P", 1, d1_read, 2, 2),
            ("yb1", 0, "S", 0, yb_read, J, 2),
            ("d2_0", 1, "P", 1, d2_read, 8, 4),
            ("cb1", 0, "F", -1, h_done, FPAIRS, 2),
            ("d2_1", 1, "P", 1, d2_read, 8, 8),
            ("cb2", 0, "F", -1, h_done, FPAIRS, 3),
            ("cb3", 0, "F", -1, h_done, FPAIRS, 4),
            ("yb2", 1, "S", 0, yb_read, J, 3),
            ("cb4", 0, "F", -1, h_done, FPAIRS, 5),
        ]
        PLACE = {u[0]: i for i, u in enumerate(USES)}

        def bank(name):
            return work[USES[PLACE[name]][1]]

        def stages(g):
            if g.it is not None:
                return "PSFT"
            n = g.base
            return "".join(c for c, m in (("P", n + 1), ("S", n), ("F", n - 1), ("T", n - 2)) if 0 <= m < NG)

        def last_reader(name, g):
            i, body = PLACE[name], g
            while True:
                i -= 1
                if i < 0:
                    i, body = len(USES) - 1, body + -1
                    if body.it is None and body.base < -1:
                        return None
                _, b, stage, off, s, per, k = USES[i]
                if b == USES[PLACE[name]][1] and stage in stages(body):
                    return s, (body + off).count(per, k)

        def run(eng, body):
            for n in (-1, 0, 1, 2):
                body(Group(n), n % 2)
            with eng.Fori(0, (NG - 4) // 2) as it:
                body(Group(3, it), 1)
                body(Group(4, it), 0)
            for n in (NG - 1, NG, NG + 1):
                body(Group(n), n % 2)

        @block.sync
        def _(sp):
            def load_weights():
                for dst, src in ((wd1, w_d1), (wbc, w_bc), (wd2, w_d2), (bd2, b_d2), (amat, a_log),
                                 (wdd, w_dd), (wout, w_out)):
                    sp.dma_start(dst[:], src).then_inc(w_in, 16)
                for dst, src in ((wrt, w_router), (lower, tri), (selb, sel), (wg, w_gate), (wu, w_up)):
                    sp.dma_start(dst[:], src).then_inc(wf_in, 16)
                sp.dma_start(wdn[:, 0:FT - 1, :], w_down[0:(FT - 1) * P, :].rearrange("(f p) d -> p f d", p=P))\
                    .then_inc(wf_in, 16)
                sp.dma_start(wdn[0:LAST, FT - 1, :], w_down[(FT - 1) * P:FEAT, :]).then_inc(wf_in, 16)

            tokens = resid.rearrange("g (t p) d -> p (g t) d", p=P)
            result = out.rearrange("g (t p) d -> p (g t) d", p=P)

            def body(g, par):
                has, q, e = stages(g), g + 1, g + -2
                rows_q = tokens[:, bass.ds(sp.snap(q.index() * TT), TT), :] if "P" in has else None
                rows_g = tokens[:, bass.ds(sp.snap(g.index() * TT), TT), :] if "S" in has else None
                rows_e = result[:, bass.ds(sp.snap(e.index() * TT), TT), :] if "T" in has else None
                if "P" in has:
                    if g.base >= 0:
                        sp.wait_ge(xn_done, q.count(2, 0))
                    sp.dma_start(xr[:], rows_q).then_inc(xr_in, 16)
                if "S" not in has and "P" in has:
                    load_weights()
                if "S" in has:
                    if "T" in has:
                        sp.wait_ge(z2_done, e.count(1, 1))
                    sp.dma_start(x1[:, par], rows_g).then_inc(res_in, 16)
                if "P" in has:
                    stored = q.held(sp, 16, 16)
                    used = [g.held(sp, SLOTS, (J - 1) * NQ + n + 1) for n in range(NQ)]
                    sp.wait_ge(d1_read, q.count(2, 2))
                    sp.dma_start(bcd[1 - par], bcs[:]).then_inc(bc_st, 16)
                    sp.wait_ge(bc_st, stored)
                    for n in range(NQ):
                        if "S" in has:
                            sp.wait_ge(dbx_full, used[n])
                        sp.dma_start(Bb[:, n * QUAD:(n + 1) * QUAD, :],
                                     bcd[1 - par, n * QUAD:(n + 1) * QUAD, :].unsqueeze(0)
                                     .broadcast_to([P, QUAD, L])).then_inc(b_in[n], 16)
                        if "S" in has:
                            sp.wait_ge(cmul_dve, used[n])
                            sp.wait_ge(cmul_pool, used[n])
                        sp.dma_start(Cb[:, n * QUAD:(n + 1) * QUAD, :],
                                     bcd[1 - par, NS + n * QUAD:NS + (n + 1) * QUAD, :].unsqueeze(0)
                                     .broadcast_to([P, QUAD, L])).then_inc(c_in[n], 16)
                if "T" in has:
                    sp.wait_ge(out_done, e.count(2, 2))
                    sp.dma_start(rows_e, ob[:]).then_inc(out_st, 16)

            run(sp, body)
            sp.wait_ge(out_st, 16 * NG)

        @block.tensor
        def _(pe):
            mm = nc.tensor.matmul

            def turn(dst, src, start, stop):
                return mm(dst, src, idn[:], start=start, stop=stop, is_transpose=True, skip_group_check=True)

            def take(name, g):
                w = last_reader(name, g)
                if w is not None:
                    pe.wait_ge(w[0], w[1])

            def body(g, par):
                has, q, f, e = stages(g), g + 1, g + -1, g + -2
                qar = 1 - par

                def xnorm_turn():
                    pe.wait_ge(xn_done, q.count(2, 2))
                    take("xnT", g)
                    w = bank("xnT")[:].rearrange("p (k t) -> p k t", k=KD)
                    for k in range(KD):
                        for t in range(TT):
                            last = turn(w[:, k, t * P:(t + 1) * P], xn[:, t, k * P:(k + 1) * P], True, True)
                    last.then_inc(xnT_ps, 1)

                def in_proj(i):
                    if i == 0:
                        pe.wait_ge(xnT_done, q.count(2, 2))
                    take(f"in{i}", g)
                    w = bank(f"in{i}")[:].rearrange("p (h t) -> p h t", h=2)
                    for h in range(2):
                        j = 2 * i + h
                        for k in range(KD):
                            last = mm(w[:, h, :], wxin[:, k, j * P:(j + 1) * P], xnT[:, qar, k, :],
                                      start=(k == 0), stop=(k == KD - 1))
                    last.then_inc(in_ps, 1)

                def skip(i):
                    take(f"skip{i}", g)
                    w = bank(f"skip{i}")[:].rearrange("p (h t) -> p h t", h=2)
                    for h in range(2):
                        j = J + 2 * i + h
                        for k in range(KD):
                            last = mm(w[:, h, :], wxin[:, k, j * P:(j + 1) * P], xnT[:, par, k, :],
                                      start=(k == 0), stop=(k == KD - 1))
                    last.then_inc(skip_ps, 1)

                def d1():
                    if g.it is None and g.base == -1:
                        pe.wait_ge(w_in, 16 * 7)
                    pe.wait_ge(xa_done, q.count(1, 1))
                    take("d1", g)
                    w = bank("d1")
                    for j in range(J):
                        mm(w[:, 0:L], wd1[:, j, :], xa[:, qar, j, :], start=(j == 0), stop=(j == J - 1))
                    for j in range(J):
                        last = mm(w[0:2 * NS, L:2 * L], wbc[:, j, :], xa[:, qar, j, :],
                                  start=(j == 0), stop=(j == J - 1))
                    last.then_inc(d1_ps, 1)

                def d2(i):
                    if i == 0:
                        pe.wait_ge(d1_read, q.count(2, 1))
                    take(f"d2_{i}", g)
                    w = bank(f"d2_{i}")[:].rearrange("p (h t) -> p h t", h=2)
                    for h in range(2):
                        j = 2 * i + h
                        last = mm(w[:, h, :], wd2[:, j * P:(j + 1) * P], r1[:], start=True, stop=True)
                    last.then_inc(d2_ps, 1)

                def y_back(gr, gpar, j):
                    pe.wait_ge(yT_copied, gr.count(J, j + 1))
                    take(f"yb{j}", g)
                    w = bank(f"yb{j}")
                    for t in range(TT):
                        last = turn(w[:, t * P:(t + 1) * P], yTs[:, j % 2, t, :], True, True)
                    last.then_inc(yb_ps, 1)

                def out_proj():
                    if g.it is None and g.base == 1:
                        pe.wait_ge(wf_in, 16 * 7)
                        pe.wait_ge(prep_wout, 2)
                    pe.wait_ge(yg_done, f.count(J, J))
                    take("outp", g)
                    w = bank("outp")[:].rearrange("p (t d) -> p t d", t=TT)
                    for t in range(TT):
                        for j in range(J):
                            last = mm(w[:, t, :], yg[:, j, t * P:(t + 1) * P], wout[:, j, :],
                                      start=(j == 0), stop=(j == J - 1))
                    last.then_inc(outp_ps, 1)

                def x1_turn():
                    pe.wait_ge(x1_done, f.count(2, 2))
                    take("x1T", g)
                    w = bank("x1T")[:].rearrange("p (k t) -> p k t", k=KD)
                    for k in range(KD):
                        for t in range(TT):
                            last = turn(w[:, k, t * P:(t + 1) * P], x1[:, qar, t, k * P:(k + 1) * P], True, True)
                    last.then_inc(x1T_ps, 1)

                def router():
                    pe.wait_ge(x1T_done, f.count(1, 1))
                    take("lg", g)
                    w = bank("lg")
                    for t in range(TT):
                        for k in range(KD):
                            last = mm(w[:, t * NXS:(t + 1) * NXS], x1T[:, k, t * P:(t + 1) * P], wrt[:, k, :],
                                      start=(k == 0), stop=(k == KD - 1))
                    last.then_inc(lg_ps, 1)

                def comb_turn():
                    pe.wait_ge(rt2, f.count(RT2, RT2))
                    take("cT", g)
                    w = bank("cT")[:].bitcast(BF16)
                    for t in range(TT):
                        last = nc.tensor.transpose(w[0:3 * NXS, t * P:(t + 1) * P],
                                                   cpart[:, t].rearrange("p a b -> p (a b)"), idb[:])
                    last.then_inc(cT_ps, 1)

                def feat_cols(i, h):
                    a = (2 * i + h) * P
                    return a, min(a + P, FEAT)

                def gate(f, i):
                    if i == 0:
                        pe.wait_ge(x1T_done, f.count(1, 1))
                    if i or f.beyond(1):
                        pe.wait_ge(g_read, f.count(FPAIRS, i))
                    for h in range(2):
                        a, b = feat_cols(i, h)
                        for k in range(KD):
                            last = mm(gps[0:b - a, h, :], wg[:, k, a:b], x1T[:, k, :],
                                      start=(k == 0), stop=(k == KD - 1))
                    last.then_inc(g_ps, 1)

                def up(f, i):
                    if i == 0:
                        pe.wait_ge(x1T_done, f.count(1, 1))
                    if i or f.beyond(1):
                        pe.wait_ge(u_read, f.count(FPAIRS, i))
                    for h in range(2):
                        a, b = feat_cols(i, h)
                        for k in range(KD):
                            last = mm(ups[0:b - a, h, :], wu[:, k, a:b], x1T[:, k, :],
                                      start=(k == 0), stop=(k == KD - 1))
                    last.then_inc(u_ps, 1)

                def spread(f, i):
                    if i == 0:
                        pe.wait_ge(cT_done, f.count(1, 1))
                    take(f"cb{i}", g)
                    w = bank(f"cb{i}")[:].rearrange("p (h t) -> p h t", h=2)
                    for h in range(2):
                        a, b = feat_cols(i, h)
                        last = mm(w[0:b - a, h, :], selb[:, a:b], cT[:], start=True, stop=True)
                    last.then_inc(cb_ps, 1)

                def down(f, i):
                    pe.wait_ge(h_done, f.count(FPAIRS, i + 1))
                    if i == 0 and f.beyond(1):
                        pe.wait_ge(z2_done, f.count(1, 0))
                    for h in range(2):
                        rows = feat_cols(i, h)[1] - feat_cols(i, h)[0]
                        for t in range(TT):
                            first = i == 0 and h == 0
                            last = mm(ops[:, t, :], hh[0:rows, i % HRING, h, t * P:(t + 1) * P], wdn[0:rows, 2 * i + h, :],
                                      start=(first and t == 0), stop=(i == FPAIRS - 1 and h == 1),
                                      skip_group_check=True)
                    last.then_inc(dn_ps, 1)

                def sum_states(gr, k):
                    j, first, final = k // PJ, k % PJ == 0, k % PJ == PJ - 1
                    if first and (j or gr.beyond(1)):
                        pe.wait_ge(yT_copied, gr.count(J, j))
                    if k % 2 == 0:
                        pe.wait_ge(cmul_dve, gr.count(SLOTS, k // 2 + 1))
                    else:
                        pe.wait_ge(cmul_pool, gr.count(SLOTS, k // 2 + 1))
                    for n in range(2):
                        for t in range(TT):
                            last = turn(yT[:, j % 2, t, :], pr[:, k % 4, n, t * P:(t + 1) * P],
                                        first and n == 0 and t == 0, final and n == 1)
                    last.then_inc(summed, 1)

                work_of = [
                    (0, "T", lambda: up(e, 5)),
                    (0, "S", lambda: skip(0)),
                    (0, "T", lambda: spread(e, 5)),
                    (1, "S", lambda: skip(1)),
                    (2, "T", lambda: down(e, 4)),
                    (2, "F", lambda: y_back(f, qar, 3)),
                    (3, "T", lambda: gate(e, 6)),
                    (4, "F", lambda: out_proj()),
                    (4, "T", lambda: up(e, 6)),
                    (5, "T", lambda: spread(e, 6)),
                    (8, "P", lambda: xnorm_turn()),
                    (8, "T", lambda: down(e, 5)),
                    (9, "F", lambda: (x1_turn(), gate(f, 0))),
                    (10, "F", lambda: router()),
                    (10, "T", lambda: down(e, 6)),
                    (10, "P", lambda: in_proj(0)),
                    (12, "F", lambda: up(f, 0)),
                    (14, "P", lambda: in_proj(1)),
                    (14, "F", lambda: (gate(f, 1), up(f, 1))),
                    (15, "S", lambda: y_back(g, par, 0)),
                    (17, "F", lambda: (gate(f, 2), comb_turn())),
                    (18, "F", lambda: (up(f, 2), spread(f, 0))),
                    (19, "F", lambda: gate(f, 3)),
                    (20, "P", lambda: d1()),
                    (21, "S", lambda: y_back(g, par, 1)),
                    (21, "P", lambda: d2(0)),
                    (21, "F", lambda: spread(f, 1)),
                    (22, "F", lambda: down(f, 0)),
                    (22, "P", lambda: d2(1)),
                    (24, "F", lambda: (spread(f, 2), up(f, 3))),
                    (26, "F", lambda: (down(f, 1), gate(f, 4), spread(f, 3), up(f, 4))),
                    (27, "S", lambda: y_back(g, par, 2)),
                    (28, "F", lambda: (spread(f, 4), down(f, 2), gate(f, 5))),
                    (30, "F", lambda: down(f, 3)),
                ]
                for s in range(2 * SLOTS):
                    for half, stage, do in work_of:
                        if half == s and any(c in has for c in stage):
                            do()
                    if "S" in has and s >= 2:
                        sum_states(g, s - 2)
                    if "F" in has and s < 2:
                        sum_states(f, PAIRS - 2 + s)

            pe.wait_ge(w0_in, 16 * 5)
            run(pe, body)

        @block.scalar
        def _(act):
            af = nc.scalar.activation
            for dst, src in ((wxin, w_xin), (idn, ident), (normw, norm_w), (convw, conv_w), (convb, conv_b)):
                act.dma_start(dst[:], src).then_inc(w0_in, 16)
            act.wait_ge(prep, PREP)

            def body(g, par):
                has, q, f, e = stages(g), g + 1, g + -1, g + -2
                qar = 1 - par

                def exp_alog():
                    if g.it is None and g.base == -1:
                        act.wait_ge(w_in, 16 * 7)
                        af(amat[:], amat[:], ACT.Exp).then_inc(prep_act, 1)

                def mean_square():
                    act.wait_ge(xr_in, q.count(16, 16))
                    for t in range(TT):
                        if t or g.base >= 0:
                            act.wait_ge(squares, q.count(2, t))
                        af(sqd[:], xr[:, t, :], ACT.Square, scale=float(D) ** -0.5,
                           accum_out=mv[:, 0, t, 1:2]).then_inc(squares, 1)

                def take_roots():
                    if "P" in has:
                        act.wait_ge(squares, q.count(2, 2))
                    if "F" in has:
                        act.wait_ge(ln1_stat, f.count(4, 4))
                    af(root[:, 0:2, :], mv[:, 0:2, :, 1], ACT.Sqrt, bias=eps[:]).then_inc(roots, 1)

                def normalise():
                    act.wait_ge(inverses, g.count(1, 2))
                    if g.base >= 0:
                        act.wait_ge(xnT_ps, q.count(1, 0))
                    for t in range(TT):
                        af(xn[:, t, :], xr[:, t, :], ACT.Copy, scale=inv[:, 0, t:t + 1]).then_inc(xn_done, 1)

                def copy_xnT():
                    act.wait_ge(xnT_ps, q.count(1, 1))
                    w = bank("xnT")[:].rearrange("p (k t) -> p k t", k=KD)
                    for k in range(KD):
                        af(xnT[:, qar, k, :], w[:, k, :], ACT.Copy, scale=normw[:, k:k + 1]).then_inc(xnT_done, 1)

                def conv_first(i):
                    act.wait_ge(in_ps, q.count(2, i + 1))
                    if i == 0 and g.base >= 0:
                        act.wait_ge(xa_done, q.count(1, 0))
                    w = bank(f"in{i}")[:].rearrange("p (h t) -> p h t", h=2)
                    for h in range(2):
                        j = 2 * i + h
                        af(xin[:, j, TAPS - 1:], w[:, h, :], ACT.Copy).then_inc(conv_in, 1)
                        af(xa[:, qar, j, :], w[:, h, :], ACT.Identity, bias=convb[:, j:j + 1],
                           scale=convw[:, j, TAPS - 1:TAPS]).then_inc(conv_in, 1)

                def conv_sig():
                    act.wait_ge(conv_step, q.count(12, 12))
                    af(spz[:], xa[:, qar], ACT.Tanh).then_inc(conv_tanh, 1)

                def copy_d1():
                    act.wait_ge(d1_ps, q.count(1, 1))
                    if g.base >= 0:
                        act.wait_ge(bc_st, q.count(16, 0))
                    w = bank("d1")
                    af(r1[:], w[:, 0:L], ACT.Copy).then_inc(d1_read, 1)
                    af(bcs[:], w[0:2 * NS, L:2 * L], ACT.Copy).then_inc(d1_read, 1)

                def softplus_parts(i):
                    act.wait_ge(d2_ps, q.count(2, i + 1))
                    if i == 0:
                        act.wait_ge(xa_done, q.count(1, 1))
                        if g.base >= 0:
                            act.wait_ge(dbx_full, g.count(SLOTS, 0))
                    w = bank(f"d2_{i}")[:].rearrange("p (h t) -> p h t", h=2)
                    for h in range(2):
                        j = 2 * i + h
                        af(spz[:, j, :], w[:, h, :], ACT.Abs, bias=bd2[:, j:j + 1]).then_inc(d2_read, 1)
                        af(dx[:, qar, j, :], w[:, h, :], ACT.Relu, bias=bd2[:, j:j + 1]).then_inc(d2_read, 1)

                def softplus_exp():
                    act.wait_ge(d2_read, q.count(8, 8))
                    af(spz[:], spz[:], ACT.Exp, scale=-1.0).then_inc(sp_exp, 1)

                def softplus_log():
                    act.wait_ge(sp_exp, q.count(1, 1))
                    af(dlt[:, qar], spz[:], ACT.Ln, bias=1.0).then_inc(sp_ln, 1)

                def skip_sig(i):
                    act.wait_ge(skip_ps, g.count(2, i + 1))
                    if "T" in has:
                        act.wait_ge(yg_done, e.count(J, J))
                    af(sk[:, par, 2 * i:2 * i + 2, :], bank(f"skip{i}")[:].rearrange("p (h t) -> p h t", h=2), ACT.Tanh,
                       scale=0.5).then_inc(skip_tanh, 1)

                def copy_yT(gr, j):
                    act.wait_ge(summed, gr.count(PAIRS, PJ * (j + 1)))
                    if j >= 2 or gr.beyond(1):
                        act.wait_ge(yb_ps, gr.count(J, j - 1))
                    af(yTs[:, j % 2], yT[:, j % 2], ACT.Copy).then_inc(yT_copied, 1)

                def decay(k):
                    j, m = k // PJ, k % 2
                    if k == 0:
                        if g.it is None and g.base == 0:
                            act.wait_ge(prep_act, 2)
                        act.wait_ge(dlt_done, g.count(1, 1))
                    if k >= 2 or g.beyond(1):
                        if m == 0:
                            act.wait_ge(cmul_dve, g.count(SLOTS, k // 2))
                        else:
                            act.wait_ge(scan_done, g.count(PAIRS, k - 1))
                    for n in range(2):
                        ns = 2 * (k % PJ) + n
                        lo = m
                        ins = af(dA[m][:, n, lo:], dlt[:, par, j, lo:], ACT.Exp,
                                 scale=amat[:, j, ns:ns + 1])
                    ins.then_inc(dA_full, 1)

                def take_root2():
                    act.wait_ge(ln2_stat, e.count(4, 4))
                    af(root[:, 2, :], mv[:, 2, :, 1], ACT.Sqrt, bias=eps[:]).then_inc(ln2_root, 1)

                def copy_x1T():
                    act.wait_ge(x1T_ps, f.count(1, 1))
                    af(x1T[:].rearrange("p k t -> p (k t)"), bank("x1T")[:], ACT.Copy).then_inc(x1T_done, 1)

                def route_exp():
                    act.wait_ge(rt1, f.count(2, 2))
                    af(ex[:], ex[:], ACT.Exp).then_inc(rt_exp, 1)
                    w = bank("lg")[:, 0:TT * NXS].rearrange("p (t x) -> p t x", t=TT)
                    af(sgt[:], w[:, :, NX:NXS], ACT.Tanh, scale=0.5).then_inc(rt_exp, 1)

                def copy_cT():
                    act.wait_ge(cT_ps, f.count(1, 1))
                    af(cT[:], bank("cT")[:].bitcast(BF16)[0:3 * NXS, 0:L], ACT.Copy).then_inc(cT_done, 1)

                def gate_sig(f, i):
                    act.wait_ge(g_ps, f.count(FPAIRS, i + 1))
                    if i >= HRING:
                        act.wait_ge(dn_ps, f.count(FPAIRS, i - HRING + 1))
                    elif f.beyond(1):
                        held = max(n for n in range(FPAIRS) if n % HRING == i)
                        act.wait_ge(dn_ps, f.count(FPAIRS, held + 1 - FPAIRS))
                    af(hh[:, i % HRING], gps[:], ACT.Tanh, scale=0.5).then_inc(g_tanh, 1)

                work_of = [
                    (0, "T", lambda: gate_sig(e, 5)),
                    (1, "S", lambda: skip_sig(0)),
                    (2, "S", lambda: skip_sig(1)),
                    (3, "F", lambda: copy_yT(f, 3)),
                    (4, "P", lambda: mean_square()),
                    (6, "T", lambda: gate_sig(e, 6)),
                    (8, "PF", lambda: take_roots()),
                    (8, "P", lambda: normalise()),
                    (10, "P", lambda: copy_xnT()),
                    (10, "F", lambda: copy_x1T()),
                    (12, "F", lambda: route_exp()),
                    (13, "S", lambda: copy_yT(g, 0)),
                    (14, "P", lambda: conv_first(0)),
                    (14, "F", lambda: gate_sig(f, 0)),
                    (16, "F", lambda: gate_sig(f, 1)),
                    (16, "P", lambda: conv_first(1)),
                    (17, "P", lambda: exp_alog()),
                    (18, "F", lambda: copy_cT()),
                    (18, "S", lambda: copy_yT(g, 1)),
                    (18, "F", lambda: gate_sig(f, 2)),
                    (18, "P", lambda: conv_sig()),
                    (21, "P", lambda: copy_d1()),
                    (22, "F", lambda: gate_sig(f, 3)),
                    (22, "P", lambda: softplus_parts(0)),
                    (24, "P", lambda: (softplus_parts(1), softplus_exp())),
                    (26, "S", lambda: copy_yT(g, 2)),
                    (26, "P", lambda: softplus_log()),
                    (28, "F", lambda: gate_sig(f, 4)),
                    (30, "T", lambda: take_root2()),
                ]
                for s in range(2 * SLOTS):
                    for half, stage, do in work_of:
                        if half == s and any(c in has for c in stage):
                            do()
                    if "S" in has:
                        decay(s)

            run(act, body)

        @block.gpsimd
        def _(pool):
            def body(g, par):
                has, q = stages(g), g + 1
                qar = 1 - par

                def softplus_loss():
                    pool.wait_ge(sp_low, q.count(1, 1))
                    nc.gpsimd.tensor_tensor(spu[:], spz[:], spu[:], ALU.subtract).then_inc(sp_pool, 1)

                def softplus_positive():
                    pool.wait_ge(sp_pool, q.count(2, 1))
                    nc.gpsimd.tensor_tensor(spu[:], dx[:, qar], spu[:], ALU.add).then_inc(sp_pool, 1)

                def drive(gr, gpar, c):
                    j, qd = c // NQ, c % NQ
                    if c == 0:
                        pool.wait_ge(dx_done, gr.count(1, 1))
                    if j == 0:
                        pool.wait_ge(b_in[qd], gr.count(16, 16))
                    if c >= DRING or gr.beyond(1):
                        pool.wait_ge(scan_done, gr.count(PAIRS, 2 * (c - DRING + 1)))
                    nc.gpsimd.tensor_tensor(
                        dbx[:, c % DRING], dx[:, gpar, j, :].unsqueeze(1).broadcast_to([P, QUAD, L]),
                        Bb[:, qd * QUAD:(qd + 1) * QUAD, :], ALU.mult).then_inc(dbx_full, 1)

                def weigh(gr, c):
                    k, qd = 2 * c + 1, c % NQ
                    pool.wait_ge(scan_done, gr.count(PAIRS, k + 1))
                    if c < NQ:
                        pool.wait_ge(c_in[qd], gr.count(16, 16))
                    nc.gpsimd.tensor_tensor(pr[:, k % 4], pr[:, k % 4],
                                            Cb[:, qd * QUAD + 2:(qd + 1) * QUAD, :], ALU.mult)\
                        .then_inc(cmul_pool, 1)

                work_of = [
                    (25, "P", lambda: softplus_loss()),
                    (27, "P", lambda: softplus_positive()),
                ]
                for s in range(2 * SLOTS):
                    for half, stage, do in work_of:
                        if half == s and any(c in has for c in stage):
                            do()
                    if "S" in has and s % 2 == 0 and s < 2 * SLOTS - 2:
                        drive(g, par, s // 2 + 1)
                    if "S" in has and s % 2:
                        weigh(g, s // 2)
                if "P" in has:
                    drive(q, qar, 0)

            run(pool, body)

        @block.vector
        def _(dve):
            ts, tt, stt = nc.vector.tensor_scalar, nc.vector.tensor_tensor, nc.vector.scalar_tensor_tensor
            nc.vector.memset(xin[:, :, 0:TAPS - 1], 0.0).then_inc(prep, 1)
            nc.vector.memset(dA[1][:, :, 0:1], 0.0).then_inc(prep, 1)
            nc.vector.memset(eps[:], EPS).then_inc(prep, 1)
            nc.vector.memset(mv[:], 1.0).then_inc(prep, 1)
            dve.wait_ge(w0_in, 16 * 5)
            ts(convw[:], convw[:], 0.5, None, ALU.mult).then_inc(prep, 1)
            ts(convb[:], convb[:], 0.5, None, ALU.mult).then_inc(prep, 1)

            def negate_a():
                dve.wait_ge(w_in, 16 * 7)
                ts(wout[:], wout[:], 0.5, None, ALU.mult).then_inc(prep_wout, 1)
                dve.wait_ge(w0_in, 16 * 5)
                nc.vector.tensor_copy(idb[:], idn[:]).then_inc(prep_wout, 1)
                dve.wait_ge(prep_act, 1)
                ts(amat[:], amat[:], -1.0, None, ALU.mult).then_inc(prep_act, 1)

            def body(g, par):
                has, q, f, e = stages(g), g + 1, g + -1, g + -2
                qar = 1 - par

                def invert():
                    dve.wait_ge(roots, g.count(1, 2))
                    nc.vector.reciprocal(inv[:, 0:2, :], root[:, 0:2, :]).then_inc(inverses, 1)

                def conv(i):
                    for tap in range(TAPS - 1):
                        for h in range(2):
                            j = 2 * i + h
                            n = 6 * i + 2 * tap + h
                            if tap == 0:
                                dve.wait_ge(conv_in, q.count(8, 2 * j + 2))
                            else:
                                dve.wait_ge(conv_step, q.count(12, n - 1))
                            stt(xa[:, qar, j, :], xin[:, j, tap:tap + L], convw[:, j, tap:tap + 1], xa[:, qar, j, :],
                                ALU.mult, ALU.add).then_inc(conv_step, 1)

                def conv_silu():
                    dve.wait_ge(conv_tanh, q.count(1, 1))
                    stt(xa[:, qar], spz[:], 1.0, xa[:, qar], ALU.add, ALU.mult).then_inc(xa_done, 1)

                def softplus_low():
                    dve.wait_ge(sp_exp, q.count(1, 1))
                    ts(spu[:], spz[:], 1.0, -1.0, ALU.add, ALU.add).then_inc(sp_low, 1)

                def delta():
                    dve.wait_ge(sp_ln, q.count(1, 1))
                    dve.wait_ge(sp_pool, q.count(2, 2))
                    tt(dlt[:, qar], dlt[:, qar], spu[:], ALU.add).then_inc(dlt_done, 1)
                    dve.wait_ge(dlt_done, q.count(1, 1))
                    tt(dx[:, qar], dlt[:, qar], xa[:, qar], ALU.mult).then_inc(dx_done, 1)

                def skip_silu(i):
                    dve.wait_ge(skip_tanh, g.count(2, i + 1))
                    stt(sk[:, par, 2 * i:2 * i + 2, :], sk[:, par, 2 * i:2 * i + 2, :], 1.0,
                        bank(f"skip{i}")[:].rearrange("p (h t) -> p h t", h=2),
                        ALU.add, ALU.mult).then_inc(sk_done, 1)

                def y_gate(gr, gpar, j):
                    dve.wait_ge(yb_ps, gr.count(J, j + 1))
                    stt(yd[:, j % 2, :], xa[:, gpar, j, :], wdd[:, j:j + 1], bank(f"yb{j}")[:, 0:L],
                        ALU.mult, ALU.add).then_inc(yb_read, 1)
                    dve.wait_ge(yb_read, gr.count(J, j + 1))
                    if j == 0 and gr.beyond(1):
                        dve.wait_ge(outp_ps, gr.count(1, 0))
                    tt(yg[:, j, :], yd[:, j % 2, :], sk[:, gpar, j, :], ALU.mult).then_inc(yg_done, 1)

                def res_norm_stats():
                    dve.wait_ge(outp_ps, f.count(1, 1))
                    dve.wait_ge(res_in, f.count(16, 16))
                    stt(x1[:, qar], x1[:, qar], 2.0, bank("outp")[:].rearrange("p (t d) -> p t d", t=TT), ALU.mult, ALU.add).then_inc(res_sum, 1)
                    dve.wait_ge(res_sum, f.count(1, 1))
                    for t in range(TT):
                        nc.vector.bn_stats(st1[:, t, :], x1[:, qar, t, :]).then_inc(ln1_stat, 1)
                    for t in range(TT):
                        need = f.held(dve, 4, t + 1)
                        dve.wait_ge(prep, PREP)
                        dve.wait_ge(ln1_stat, need)
                        nc.vector.bn_aggr(mv[:, 1, t, :], st1[:, t, :]).then_inc(ln1_stat, 1)

                def res_norm():
                    dve.wait_ge(inverses, g.count(1, 2))
                    for t in range(TT):
                        ts(x1[:, qar, t, :], x1[:, qar, t, :], mv[:, 1, t, 0:1], inv[:, 1, t:t + 1],
                           ALU.subtract, ALU.mult).then_inc(x1_done, 1)

                def route_max():
                    dve.wait_ge(lg_ps, f.count(1, 1))
                    lg = bank("lg")[:, 0:TT * NXS].rearrange("p (t x) -> p t x", t=TT)[:, :, 0:NX]
                    nc.vector.tensor_reduce(lmax[:], lg, AX.X, ALU.max).then_inc(rt1, 1)
                    dve.wait_ge(rt1, f.count(2, 1))
                    tt(ex[:], lg, lmax[:].unsqueeze(2).broadcast_to([P, TT, NX]), ALU.subtract).then_inc(rt1, 1)

                def route_top2():
                    step = [0]

                    def then(ins):
                        step[0] += 1
                        ins.then_inc(rt2, 1)

                    def settle():
                        dve.wait_ge(rt2, f.count(RT2, step[0]))

                    other = ex[:].unsqueeze(2).broadcast_to([P, TT, NX, NX])
                    own = ex[:].unsqueeze(3).broadcast_to([P, TT, NX, NX])
                    dve.wait_ge(rt_exp, f.count(2, 2))
                    then(tt(gt[:], other, own, ALU.is_gt))
                    then(tt(eq[:], other, own, ALU.is_equal))
                    settle()
                    then(tt(eq[:], eq[:], lower[:].unsqueeze(1).broadcast_to([P, TT, NX, NX]), ALU.mult))
                    settle()
                    then(tt(gt[:], gt[:], eq[:], ALU.add))
                    settle()
                    then(nc.vector.tensor_reduce(rank[:], gt[:], AX.X, ALU.add))
                    settle()
                    then(stt(top[:], rank[:], 2.0, ex[:], ALU.is_lt, ALU.mult))
                    settle()
                    then(nc.vector.tensor_reduce(tsum[:], top[:], AX.X, ALU.add))
                    settle()
                    then(nc.vector.reciprocal(tinv[:], tsum[:]))
                    settle()
                    then(stt(comb[:, :, 0:NX], top[:], 0.5, tinv[:].unsqueeze(2).broadcast_to([P, TT, NX]),
                             ALU.mult, ALU.mult))
                    then(ts(comb[:, :, NX:NXS], sgt[:], 0.25, 0.25, ALU.mult, ALU.add))
                    settle()
                    then(nc.vector.tensor_copy(cpart[:, :, 0, :], comb[:]))
                    settle()
                    then(tt(crest[:], comb[:], cpart[:, :, 0, :], ALU.subtract))
                    settle()
                    then(nc.vector.tensor_copy(cpart[:, :, 1, :], crest[:]))
                    settle()
                    then(tt(comb[:], crest[:], cpart[:, :, 1, :], ALU.subtract))
                    settle()
                    then(nc.vector.tensor_copy(cpart[:, :, 2, :], comb[:]))
                    assert step[0] == RT2

                def glu_gate(f, i):
                    dve.wait_ge(g_tanh, f.count(FPAIRS, i + 1))
                    stt(hh[:, i % HRING], hh[:, i % HRING], 1.0, gps[:], ALU.add, ALU.mult).then_inc(g_read, 1)

                def glu_up(f, i):
                    dve.wait_ge(g_read, f.count(FPAIRS, i + 1))
                    dve.wait_ge(u_ps, f.count(FPAIRS, i + 1))
                    tt(hh[:, i % HRING], hh[:, i % HRING], ups[:], ALU.mult).then_inc(u_read, 1)

                def glu_weigh(f, i):
                    dve.wait_ge(u_read, f.count(FPAIRS, i + 1))
                    dve.wait_ge(cb_ps, f.count(FPAIRS, i + 1))
                    tt(hh[:, i % HRING], hh[:, i % HRING], bank(f"cb{i}")[:].rearrange("p (h t) -> p h t", h=2),
                       ALU.mult).then_inc(h_done, 1)

                def out_stats():
                    dve.wait_ge(dn_ps, e.count(FPAIRS, FPAIRS))
                    if e.beyond(1):
                        dve.wait_ge(out_st, e.count(16, 0))
                    tt(ob[:], x1[:, par], ops[:], ALU.add).then_inc(z2_done, 1)
                    dve.wait_ge(z2_done, e.count(1, 1))
                    for t in range(TT):
                        nc.vector.bn_stats(st2[:, t, :], ob[:, t, :]).then_inc(ln2_stat, 1)
                    for t in range(TT):
                        need = e.held(dve, 4, t + 1)
                        dve.wait_ge(prep, PREP)
                        dve.wait_ge(ln2_stat, need)
                        nc.vector.bn_aggr(mv[:, 2, t, :], st2[:, t, :]).then_inc(ln2_stat, 1)

                def out_norm():
                    dve.wait_ge(ln2_root, e.count(1, 1))
                    nc.vector.reciprocal(inv[:, 2, :], root[:, 2, :]).then_inc(ln2_inv, 1)
                    dve.wait_ge(ln2_inv, e.count(1, 1))
                    for t in range(TT):
                        ts(ob[:, t, :], ob[:, t, :], mv[:, 2, t, 0:1], inv[:, 2, t:t + 1],
                           ALU.subtract, ALU.mult).then_inc(out_done, 1)

                mul, add = ALU.mult, ALU.add

                def first_body_end():
                    if g.it is None and g.base == -1:
                        negate_a()

                def scan_even(c):
                    k = 2 * c
                    dve.wait_ge(dbx_full, g.count(SLOTS, c + 1))
                    dve.wait_ge(dA_full, g.count(PAIRS, k + 1))
                    for n in range(2):
                        ins = nc.vector.tensor_tensor_scan(dA[0][:, n, :], dA[0][:, n, :], dbx[:, c % DRING, n, :],
                                                           0.0, mul, add)
                    ins.then_inc(scan_done, 1)

                def scan_odd(c):
                    j, qd, k = c // NQ, c % NQ, 2 * c
                    dve.wait_ge(dA_full, g.count(PAIRS, k + 2))
                    if c >= 2 or g.beyond(1):
                        dve.wait_ge(summed, g.count(PAIRS, k - 2))
                    nc.vector.tensor_tensor_scan(
                        pr[:, (k + 1) % 4].rearrange("p n t -> p (n t)"), dA[1][:].rearrange("p n t -> p (n t)"),
                        dbx[:, c % DRING, 2:4, :].rearrange("p n t -> p (n t)"), 0.0, mul, add).then_inc(scan_done, 1)
                    dve.wait_ge(scan_done, g.count(PAIRS, k + 1))
                    if j == 0:
                        dve.wait_ge(c_in[qd], g.count(16, 16))
                    tt(pr[:, k % 4], dA[0][:], Cb[:, qd * QUAD:qd * QUAD + 2, :], mul).then_inc(cmul_dve, 1)

                work_of = [
                    (0, "T", lambda: (glu_gate(e, 5), glu_up(e, 5), glu_weigh(e, 5))),
                    (0, "S", lambda: skip_silu(0)),
                    (2, "S", lambda: skip_silu(1)),
                    (3, "F", lambda: y_gate(f, qar, 3)),
                    (6, "T", lambda: glu_gate(e, 6)),
                    (6, "F", lambda: res_norm_stats()),
                    (7, "T", lambda: glu_up(e, 6)),
                    (7, "PF", lambda: invert()),
                    (8, "T", lambda: glu_weigh(e, 6)),
                    (8, "F", lambda: res_norm()),
                    (11, "F", lambda: route_max()),
                    (12, "F", lambda: route_top2()),
                    (14, "F", lambda: glu_gate(f, 0)),
                    (14, "P", lambda: conv(0)),
                    (14, "F", lambda: glu_up(f, 0)),
                    (15, "F", lambda: glu_gate(f, 1)),
                    (16, "F", lambda: glu_up(f, 1)),
                    (16, "P", lambda: conv(1)),
                    (17, "S", lambda: y_gate(g, par, 0)),
                    (18, "F", lambda: glu_gate(f, 2)),
                    (19, "P", lambda: conv_silu()),
                    (19, "T", lambda: out_stats()),
                    (20, "F", lambda: glu_weigh(f, 0)),
                    (21, "S", lambda: y_gate(g, par, 1)),
                    (22, "F", lambda: (glu_weigh(f, 1), glu_up(f, 2))),
                    (23, "F", lambda: glu_gate(f, 3)),
                    (24, "P", lambda: softplus_low()),
                    (24, "F", lambda: glu_up(f, 3)),
                    (25, "F", lambda: glu_weigh(f, 2)),
                    (26, "F", lambda: glu_weigh(f, 3)),
                    (27, "P", lambda: first_body_end()),
                    (28, "S", lambda: y_gate(g, par, 2)),
                    (28, "F", lambda: glu_gate(f, 4)),
                    (29, "F", lambda: glu_up(f, 4)),
                    (30, "P", lambda: delta()),
                    (30, "T", lambda: out_norm()),
                    (31, "F", lambda: glu_weigh(f, 4)),
                ]
                for s in range(2 * SLOTS):
                    for half, stage, do in work_of:
                        if half == s and any(c in has for c in stage):
                            do()
                    if "S" in has:
                        (scan_odd if s % 2 else scan_even)(s // 2)

            run(dve, body)


_OUT = (16, 256, 256)


def kernel(**inputs):
    import ml_dtypes
    import numpy as np
    import concourse.bacc as _bacc
    from concourse import mybir as _mybir
    from concourse.bass_utils import run_bass_kernel_spmd as _run

    a = {k: np.asarray(v) for k, v in inputs.items()}
    P = 128

    def rows(w):
        n = w.shape[0] // P
        return np.ascontiguousarray(w.reshape(n, P, -1).swapaxes(0, 1))

    attn = lambda n: a["L0_attn_" + n]
    ffn = lambda n: a["L0_ffn_" + n]
    NX, D, H = ffn("w_gate").shape
    HS = ffn("shw_gate").shape[1]
    FEAT = NX * H + HS
    owner = np.concatenate([np.repeat(np.arange(NX), H), np.full(HS, NX)])
    sel = (owner[None, :] == (np.arange(3 * (NX + 1)) % (NX + 1))[:, None]).astype(np.float32)
    tri = np.ascontiguousarray(np.broadcast_to(np.tril(np.ones((NX, NX), np.float32), -1), (P, NX, NX)))
    side = lambda w, sh: np.concatenate([w.transpose(1, 0, 2).reshape(D, NX * H), sh], axis=1)
    arrays = {
        "resid": attn("resid"),
        "w_xin": rows(np.concatenate([attn("W_in"), attn("W_skip")], axis=0).T),
        "norm_w": rows(attn("norm_w"))[:, :, 0],
        "conv_w": rows(attn("conv_w")),
        "conv_b": rows(attn("conv_b"))[:, :, 0],
        "w_d1": rows(attn("W_d1").T),
        "w_d2": attn("W_d2").T,
        "b_d2": rows(attn("b_d2"))[:, :, 0],
        "w_bc": rows(np.concatenate([attn("W_Bm"), attn("W_Cm")], axis=0).T),
        "a_log": rows(attn("A_log")),
        "w_dd": rows(attn("W_D"))[:, :, 0],
        "w_out": rows(attn("W_out").T),
        "w_router": rows(np.concatenate([ffn("gate_w"), ffn("shgate_w")[None, :]], axis=0).T),
        "w_gate": rows(side(ffn("w_gate"), ffn("shw_gate"))),
        "w_up": rows(side(ffn("w_up"), ffn("shw_up"))),
        "w_down": np.concatenate([ffn("w_down").reshape(NX * H, D), ffn("shw_down")], axis=0),
        "sel": sel.astype(ml_dtypes.bfloat16),
        "tri": tri,
        "ident": np.eye(P, dtype=np.float32),
    }
    arrays = {f"{k}_dram": np.ascontiguousarray(v) for k, v in arrays.items()}
    nc = _bacc.Bacc("TRN2", target_bir_lowering=False, num_devices=1)
    args = [nc.dram_tensor(k, v.shape, _mybir.dt.from_np(v.dtype), kind="ExternalInput").ap()
            for k, v in arrays.items()]
    args.append(nc.dram_tensor("out_dram", _OUT, _mybir.dt.float32, kind="ExternalOutput").ap())
    build(nc, *args)
    r = _run(nc, [arrays], core_ids=[0])
    return r.results[0]["out_dram"]
```

```python
from contextlib import ExitStack

import concourse.bass as bass
from concourse import mybir

ALU = mybir.AluOpType
ACT = mybir.ActivationFunctionType
AX = mybir.AxisListType
F32 = mybir.dt.float32
F32R = mybir.dt.float32r
BF16 = mybir.dt.bfloat16

P = 128
EPS = 1e-5


class Group:

    def __init__(self, base, it=None):
        self.base, self.it = base, it

    def __add__(self, d):
        return Group(self.base + d, self.it)

    def count(self, per, k):
        fixed = self.base * per + k
        return fixed if self.it is None else self.it * (2 * per) + fixed

    def held(self, eng, per, k):
        if self.it is None:
            return self.count(per, k)
        reg = eng.alloc_register()
        eng.reg_mov(reg, self.count(per, k))
        return eng.snap(reg)

    def beyond(self, n):
        return self.base >= n

    def index(self):
        return self.base if self.it is None else self.it * 2 + self.base


def build(nc, resid, w_xin, norm_w, conv_w, conv_b, w_d1, w_d2, b_d2, w_bc, a_log, w_dd, w_out,
          w_router, w_gate, w_up, w_down, sel, tri, ident, out):
    NG, L, D = resid.shape
    TT = L // P
    KD = D // P
    E = w_dd.shape[0] * w_dd.shape[1]
    J = E // P
    NS = a_log.shape[2]
    R = w_d2.shape[0]
    TAPS = conv_w.shape[2]
    NX = w_router.shape[2] - 1
    NXS = NX + 1
    FEAT = w_gate.shape[2]
    FT = (FEAT + P - 1) // P
    FPAIRS = FT // 2
    LAST = FEAT - (FT - 1) * P
    QUAD = 4
    NQ = NS // QUAD
    SLOTS = J * NQ
    PAIRS = 2 * SLOTS
    DRING = 2
    HRING = 4
    PJ = NS // 2
    assert TT == 2 and KD == 2 and J == 4 and FT == 14 and TAPS == 4 and R == P and NX == 8

    with ExitStack() as ctx:
        def sb(name, shape, dt=F32):
            return ctx.enter_context(nc.sbuf_tensor(name, shape, dt))

        def ps(name, shape, dt=F32):
            return ctx.enter_context(nc.psum_tensor(name, shape, dt))

        def sem(name):
            return ctx.enter_context(nc.semaphore(name))

        wxin = sb("wxin", [P, KD, 2 * E])
        normw = sb("normw", [P, KD])
        convw = sb("convw", [P, J, TAPS])
        convb = sb("convb", [P, J])
        wd1 = sb("wd1", [P, J, R])
        wd2 = sb("wd2", [R, E])
        bd2 = sb("bd2", [P, J])
        wbc = sb("wbc", [P, J, 2 * NS])
        amat = sb("amat", [P, J, NS])
        wdd = sb("wdd", [P, J])
        wout = sb("wout", [P, J, D])
        wrt = sb("wrt", [P, KD, NXS])
        wgh = sb("wgh", [P, KD, FEAT], F32R)
        wgl = sb("wgl", [P, KD, FEAT], F32R)
        wuh = sb("wuh", [P, KD, FEAT], F32R)
        wul = sb("wul", [P, KD, FEAT], F32R)
        wdn = sb("wdn", [P, FT, D])
        selb = sb("selb", [3 * NXS, FEAT], BF16)
        lower = sb("lower", [P, NX, NX])
        idn = sb("idn", [P, P])
        idb = sb("idb", [P, P], BF16)
        eps = sb("eps", [P, 1])

        xr = sb("xr", [P, TT, D])
        sqd = sb("sqd", [P, D])
        mv = sb("mv", [P, 3, TT, 2])
        root = sb("root", [P, 3, TT])
        inv = sb("inv", [P, 3, TT])
        xnT = sb("xnT", [P, KD, L])
        xin = sb("xin", [P, J, TAPS - 1 + L])
        xa = sb("xa", [P, 2, J, L])
        r1 = sb("r1", [P, L])
        bcs = sb("bcs", [2 * NS, L])
        spz = sb("spz", [P, J, L])
        spu = xin[:, :, TAPS - 1:]
        dlt = sb("dlt", [P, 2, J, L])
        dx = sb("dx", [P, 2, J, L])
        sk = sb("sk", [P, J, L])

        Bb = sb("Bb", [P, NS, L])
        Cb = sb("Cb", [P, NS, L])
        dbx = sb("dbx", [P, DRING, QUAD, L])
        pr = sb("pr", [P, 4, 2, L])
        yTs = sb("yTs", [P, 2, TT, P])
        yg = sb("yg", [P, J, L])

        x1 = sb("x1", [P, 2, TT, D])
        st1 = sb("st1", [P, TT, 6])
        st2 = sb("st2", [P, TT, 6])
        x1Th = sb("x1Th", [P, KD, L], F32R)
        x1Tl = sb("x1Tl", [P, KD, L], F32R)
        lmax = sb("lmax", [P, TT])
        ex = sb("ex", [P, TT, NX])
        sgt = sb("sgt", [P, TT, 1])
        gt = sb("gt", [P, TT, NX, NX])
        eq = sb("eq", [P, TT, NX, NX])
        rank = eq[:, :, 0, :]
        top = sb("top", [P, TT, NX])
        tsum = sb("tsum", [P, TT])
        tinv = sb("tinv", [P, TT])
        comb = sb("comb", [P, TT, NXS])
        cpart = sb("cpart", [P, TT, 3, NXS], BF16)
        crest = gt[:].rearrange("p t a b -> p (t a b)")[:, 0:TT * NXS].rearrange("p (t x) -> p t x", t=TT)
        cT = sb("cT", [3 * NXS, L], BF16)
        hh = sb("hh", [P, HRING, 2, L])
        ob = sb("ob", [P, TT, D])

        bcd = nc.dram_tensor("bc_scratch", [2, 2 * NS, L], F32, kind="Internal").ap()

        dA = [ps(f"dA{i}", [P, 2, L]) for i in range(2)]
        yT = ps("yT", [P, 2, TT, P])
        work = [ps(f"work{i}", [P, 512]) for i in range(2)]
        gps = ps("gps", [P, 2, L])
        ups = ps("ups", [P, 2, L])
        ops = ps("ops", [P, TT, D])

        w0_in = sem("w0_in")
        w_in = sem("w_in")
        wgu_in = sem("wgu_in")
        wf_in = sem("wf_in")
        prep_act = sem("prep_act")
        prep = sem("prep")
        prep_wout = sem("prep_wout")
        PREP = 7
        xr_in = sem("xr_in")
        res_in = sem("res_in")
        bc_st = sem("bc_st")
        b_in = [sem(f"b_in{q}") for q in range(NQ)]
        c_in = [sem(f"c_in{q}") for q in range(NQ)]
        out_st = sem("out_st")
        squares = sem("squares")
        roots = sem("roots")
        inverses = sem("inverses")
        xn_done = sem("xn_done")
        xnT_ps = sem("xnT_ps")
        xnT_done = sem("xnT_done")
        in_ps = sem("in_ps")
        conv_in = sem("conv_in")
        conv_step = sem("conv_step")
        conv_tanh = sem("conv_tanh")
        xa_done = sem("xa_done")
        d1_ps = sem("d1_ps")
        d1_read = sem("d1_read")
        d2_ps = sem("d2_ps")
        d2_read = sem("d2_read")
        sp_exp = sem("sp_exp")
        sp_ln = sem("sp_ln")
        sp_low = sem("sp_low")
        sp_pool = sem("sp_pool")
        dlt_done = sem("dlt_done")
        dx_done = sem("dx_done")
        skip_ps = sem("skip_ps")
        skip_tanh = sem("skip_tanh")
        sk_done = sem("sk_done")
        dA_full = sem("dA_full")
        dbx_full = sem("dbx_full")
        scan_done = sem("scan_done")
        cmul_dve = sem("cmul_dve")
        cmul_pool = sem("cmul_pool")
        summed = sem("summed")
        yT_copied = sem("yT_copied")
        yb_ps = sem("yb_ps")
        yb_read = sem("yb_read")
        yg_done = sem("yg_done")
        outp_ps = sem("outp_ps")
        res_sum = sem("res_sum")
        ln1_stat = sem("ln1_stat")
        x1_done = sem("x1_done")
        x1T_ps = sem("x1T_ps")
        x1T_done = sem("x1T_done")
        x1T_low = sem("x1T_low")
        wgu_part = sem("wgu_part")
        lg_ps = sem("lg_ps")
        rt1 = sem("rt1")
        rt_exp = sem("rt_exp")
        rt2 = sem("rt2")
        RT2 = 15
        cT_ps = sem("cT_ps")
        cT_done = sem("cT_done")
        g_ps = sem("g_ps")
        g_tanh = sem("g_tanh")
        g_read = sem("g_read")
        u_ps = sem("u_ps")
        u_read = sem("u_read")
        cb_ps = sem("cb_ps")
        h_done = sem("h_done")
        dn_ps = sem("dn_ps")
        z2_done = sem("z2_done")
        ln2_stat = sem("ln2_stat")
        ln2_root = sem("ln2_root")
        ln2_inv = sem("ln2_inv")
        out_done = sem("out_done")

        staged = hh[:].rearrange("p r h t -> p (r h t)")[:, 0:FEAT]
        block = ctx.enter_context(nc.Block())

        USES = [
            ("skip0", 1, "S", 0, sk_done, 2, 1),
            ("yb3", 0, "F", -1, yb_read, J, 4),
            ("outp", 1, "F", -1, res_sum, 1, 1),
            ("skip1", 0, "S", 0, sk_done, 2, 2),
            ("cb6", 1, "T", -2, h_done, FPAIRS, 7),
            ("x1T", 1, "F", -1, x1T_low, 1, 1),
            ("xnT", 0, "P", 1, xnT_done, 2, 2),
            ("lg", 1, "F", -1, rt_exp, 2, 2),
            ("in0", 1, "P", 1, conv_in, 8, 4),
            ("cT", 1, "F", -1, cT_done, 1, 1),
            ("in1", 0, "P", 1, conv_in, 8, 8),
            ("yb0", 1, "S", 0, yb_read, J, 1),
            ("cb0", 0, "F", -1, h_done, FPAIRS, 1),
            ("d1", 1, "P", 1, d1_read, 2, 2),
            ("yb1", 0, "S", 0, yb_read, J, 2),
            ("d2_0", 1, "P", 1, d2_read, 8, 4),
            ("cb1", 0, "F", -1, h_done, FPAIRS, 2),
            ("d2_1", 0, "P", 1, d2_read, 8, 8),
            ("cb2", 1, "F", -1, h_done, FPAIRS, 3),
            ("cb3", 1, "F", -1, h_done, FPAIRS, 4),
            ("yb2", 0, "S", 0, yb_read, J, 3),
            ("cb4", 1, "F", -1, h_done, FPAIRS, 5),
            ("cb5", 0, "F", -1, h_done, FPAIRS, 6),
        ]
        PLACE = {u[0]: i for i, u in enumerate(USES)}

        def bank(name):
            return work[USES[PLACE[name]][1]]

        def stages(g):
            if g.it is not None:
                return "PSFT"
            n = g.base
            return "".join(c for c, m in (("P", n + 1), ("S", n), ("F", n - 1), ("T", n - 2)) if 0 <= m < NG)

        def last_reader(name, g):
            i, body = PLACE[name], g
            while True:
                i -= 1
                if i < 0:
                    i, body = len(USES) - 1, body + -1
                    if body.it is None and body.base < -1:
                        return None
                _, b, stage, off, s, per, k = USES[i]
                if b == USES[PLACE[name]][1] and stage in stages(body):
                    return s, (body + off).count(per, k)

        def run(eng, body):
            for n in (-1, 0, 1, 2):
                body(Group(n), n % 2)
            with eng.Fori(0, (NG - 4) // 2) as it:
                body(Group(3, it), 1)
                body(Group(4, it), 0)
            for n in (NG - 1, NG, NG + 1):
                body(Group(n), n % 2)

        @block.sync
        def _(sp):
            def load_weights():
                for dst, src in ((wd1, w_d1), (wbc, w_bc), (wd2, w_d2), (bd2, b_d2), (amat, a_log),
                                 (wdd, w_dd), (wout, w_out)):
                    sp.dma_start(dst[:], src).then_inc(w_in, 16)
                for dst, src in ((wrt, w_router), (lower, tri), (selb, sel)):
                    sp.dma_start(dst[:], src).then_inc(wf_in, 16)
                sp.dma_start(wdn[:, 0:FT - 1, :], w_down[0:(FT - 1) * P, :].rearrange("(f p) d -> p f d", p=P))\
                    .then_inc(wf_in, 16)
                sp.dma_start(wdn[0:LAST, FT - 1, :], w_down[(FT - 1) * P:FEAT, :]).then_inc(wf_in, 16)

            tokens = resid.rearrange("g (t p) d -> p (g t) d", p=P)
            result = out.rearrange("g (t p) d -> p (g t) d", p=P)

            def body(g, par):
                has, q, e = stages(g), g + 1, g + -2
                rows_q = tokens[:, bass.ds(sp.snap(q.index() * TT), TT), :] if "P" in has else None
                rows_g = tokens[:, bass.ds(sp.snap(g.index() * TT), TT), :] if "S" in has else None
                rows_e = result[:, bass.ds(sp.snap(e.index() * TT), TT), :] if "T" in has else None
                if "P" in has:
                    if g.base >= 0:
                        sp.wait_ge(xnT_ps, q.count(1, 0))
                    sp.dma_start(xr[:], rows_q).then_inc(xr_in, 16)
                if "S" not in has and "P" in has:
                    load_weights()
                if "S" in has:
                    if "T" in has:
                        sp.wait_ge(z2_done, e.count(1, 1))
                    sp.dma_start(x1[:, par], rows_g).then_inc(res_in, 16)
                if g.it is None and g.base == 0:
                    for n in range(2 * KD):
                        if n:
                            sp.wait_ge(wgu_part, 2 * n)
                        sp.dma_start(staged, (w_gate, w_up)[n // KD][:, n % KD, :]).then_inc(wgu_in, 16)
                if "P" in has:
                    stored = q.held(sp, 16, 16)
                    used = [g.held(sp, SLOTS, (J - 1) * NQ + n + 1) for n in range(NQ)]
                    sp.wait_ge(d1_read, q.count(2, 2))
                    sp.dma_start(bcd[1 - par], bcs[:]).then_inc(bc_st, 16)
                    sp.wait_ge(bc_st, stored)
                    for n in range(NQ):
                        if "S" in has:
                            sp.wait_ge(dbx_full, used[n])
                        sp.dma_start(Bb[:, n * QUAD:(n + 1) * QUAD, :],
                                     bcd[1 - par, n * QUAD:(n + 1) * QUAD, :].unsqueeze(0)
                                     .broadcast_to([P, QUAD, L])).then_inc(b_in[n], 16)
                        if "S" in has:
                            sp.wait_ge(cmul_dve, used[n])
                            sp.wait_ge(cmul_pool, used[n])
                        sp.dma_start(Cb[:, n * QUAD:(n + 1) * QUAD, :],
                                     bcd[1 - par, NS + n * QUAD:NS + (n + 1) * QUAD, :].unsqueeze(0)
                                     .broadcast_to([P, QUAD, L])).then_inc(c_in[n], 16)
                if "T" in has:
                    sp.wait_ge(out_done, e.count(2, 2))
                    sp.dma_start(rows_e, ob[:]).then_inc(out_st, 16)

            run(sp, body)
            sp.wait_ge(out_st, 16 * NG)

        @block.tensor
        def _(pe):
            mm = nc.tensor.matmul

            def turn(dst, src, start, stop):
                return mm(dst, src, idn[:], start=start, stop=stop, is_transpose=True, skip_group_check=True)

            def take(name, g):
                w = last_reader(name, g)
                if w is not None:
                    pe.wait_ge(w[0], w[1])

            def body(g, par):
                has, q, f, e = stages(g), g + 1, g + -1, g + -2
                qar = 1 - par

                def xnorm_turn():
                    pe.wait_ge(xn_done, q.count(2, 2))
                    take("xnT", g)
                    w = bank("xnT")[:].rearrange("p (k t) -> p k t", k=KD)
                    for k in range(KD):
                        for t in range(TT):
                            last = turn(w[:, k, t * P:(t + 1) * P], xr[:, t, k * P:(k + 1) * P], True, True)
                    last.then_inc(xnT_ps, 1)

                def in_proj(i):
                    if i == 0:
                        pe.wait_ge(xnT_done, q.count(2, 2))
                    take(f"in{i}", g)
                    w = bank(f"in{i}")[:].rearrange("p (h t) -> p h t", h=2)
                    for h in range(2):
                        j = 2 * i + h
                        for k in range(KD):
                            last = mm(w[:, h, :], wxin[:, k, j * P:(j + 1) * P], xnT[:, k, :],
                                      start=(k == 0), stop=(k == KD - 1))
                    last.then_inc(in_ps, 1)

                def skip(i):
                    take(f"skip{i}", g)
                    w = bank(f"skip{i}")[:].rearrange("p (h t) -> p h t", h=2)
                    for h in range(2):
                        j = J + 2 * i + h
                        for k in range(KD):
                            last = mm(w[:, h, :], wxin[:, k, j * P:(j + 1) * P], xnT[:, k, :],
                                      start=(k == 0), stop=(k == KD - 1))
                    last.then_inc(skip_ps, 1)

                def d1():
                    if g.it is None and g.base == -1:
                        pe.wait_ge(w_in, 16 * 7)
                    pe.wait_ge(xa_done, q.count(1, 1))
                    take("d1", g)
                    w = bank("d1")
                    for j in range(J):
                        mm(w[:, 0:L], wd1[:, j, :], xa[:, qar, j, :], start=(j == 0), stop=(j == J - 1))
                    for j in range(J):
                        last = mm(w[0:2 * NS, L:2 * L], wbc[:, j, :], xa[:, qar, j, :],
                                  start=(j == 0), stop=(j == J - 1))
                    last.then_inc(d1_ps, 1)

                def d2(i):
                    if i == 0:
                        pe.wait_ge(d1_read, q.count(2, 1))
                    take(f"d2_{i}", g)
                    w = bank(f"d2_{i}")[:].rearrange("p (h t) -> p h t", h=2)
                    for h in range(2):
                        j = 2 * i + h
                        last = mm(w[:, h, :], wd2[:, j * P:(j + 1) * P], r1[:], start=True, stop=True)
                    last.then_inc(d2_ps, 1)

                def y_back(gr, gpar, j):
                    pe.wait_ge(yT_copied, gr.count(J, j + 1))
                    take(f"yb{j}", g)
                    w = bank(f"yb{j}")
                    for t in range(TT):
                        last = turn(w[:, t * P:(t + 1) * P], yTs[:, j % 2, t, :], True, True)
                    last.then_inc(yb_ps, 1)

                def out_proj():
                    if g.it is None and g.base == 1:
                        pe.wait_ge(wf_in, 16 * 5)
                        pe.wait_ge(wgu_part, 4 * KD)
                        pe.wait_ge(prep_wout, 2)
                    pe.wait_ge(yg_done, f.count(J, J))
                    take("outp", g)
                    w = bank("outp")[:].rearrange("p (t d) -> p t d", t=TT)
                    for t in range(TT):
                        for j in range(J):
                            last = mm(w[:, t, :], yg[:, j, t * P:(t + 1) * P], wout[:, j, :],
                                      start=(j == 0), stop=(j == J - 1))
                    last.then_inc(outp_ps, 1)

                def x1_turn():
                    pe.wait_ge(x1_done, f.count(2, 2))
                    take("x1T", g)
                    w = bank("x1T")[:].rearrange("p (k t) -> p k t", k=KD)
                    for k in range(KD):
                        for t in range(TT):
                            last = turn(w[:, k, t * P:(t + 1) * P], x1[:, qar, t, k * P:(k + 1) * P], True, True)
                    last.then_inc(x1T_ps, 1)

                def router():
                    pe.wait_ge(x1T_low, f.count(1, 1))
                    take("lg", g)
                    w = bank("lg")
                    for t in range(TT):
                        for k in range(KD):
                            for n, x in enumerate((x1Th, x1Tl)):
                                last = mm(w[:, t * NXS:(t + 1) * NXS], x[:, k, t * P:(t + 1) * P].bitcast(F32),
                                          wrt[:, k, :], start=(k == 0 and n == 0), stop=(k == KD - 1 and n == 1))
                    last.then_inc(lg_ps, 1)

                def comb_turn():
                    pe.wait_ge(rt2, f.count(RT2, RT2))
                    take("cT", g)
                    w = bank("cT")[:].bitcast(BF16)
                    for t in range(TT):
                        last = nc.tensor.transpose(w[0:3 * NXS, t * P:(t + 1) * P],
                                                   cpart[:, t].rearrange("p a b -> p (a b)"), idb[:])
                    last.then_inc(cT_ps, 1)

                def feat_cols(i, h):
                    a = (2 * i + h) * P
                    return a, min(a + P, FEAT)

                def in_parts(dst, i, whi, wlo):
                    for h in range(2):
                        a, b = feat_cols(i, h)
                        for k in range(KD):
                            for n, (w, x) in enumerate(((whi, x1Th), (wlo, x1Th), (whi, x1Tl))):
                                last = mm(dst[0:b - a, h, :], w[:, k, a:b], x[:, k, :],
                                          start=(k == 0 and n == 0), stop=(k == KD - 1 and n == 2))
                    return last

                def gate(f, i):
                    if i == 0:
                        pe.wait_ge(x1T_low, f.count(1, 1))
                    if i or f.beyond(1):
                        pe.wait_ge(g_read, f.count(FPAIRS, i))
                    in_parts(gps, i, wgh, wgl).then_inc(g_ps, 1)

                def up(f, i):
                    if i == 0:
                        pe.wait_ge(x1T_low, f.count(1, 1))
                    if i or f.beyond(1):
                        pe.wait_ge(u_read, f.count(FPAIRS, i))
                    in_parts(ups, i, wuh, wul).then_inc(u_ps, 1)

                def spread(f, i):
                    if i == 0:
                        pe.wait_ge(cT_done, f.count(1, 1))
                    take(f"cb{i}", g)
                    w = bank(f"cb{i}")[:].rearrange("p (h t) -> p h t", h=2)
                    for h in range(2):
                        a, b = feat_cols(i, h)
                        last = mm(w[0:b - a, h, :], selb[:, a:b], cT[:], start=True, stop=True)
                    last.then_inc(cb_ps, 1)

                def down(f, i):
                    pe.wait_ge(h_done, f.count(FPAIRS, i + 1))
                    if i == 0 and f.beyond(1):
                        pe.wait_ge(z2_done, f.count(1, 0))
                    for h in range(2):
                        rows = feat_cols(i, h)[1] - feat_cols(i, h)[0]
                        for t in range(TT):
                            first = i == 0 and h == 0
                            last = mm(ops[:, t, :], hh[0:rows, i % HRING, h, t * P:(t + 1) * P], wdn[0:rows, 2 * i + h, :],
                                      start=(first and t == 0), stop=(i == FPAIRS - 1 and h == 1),
                                      skip_group_check=True)
                    last.then_inc(dn_ps, 1)

                def sum_states(gr, k):
                    j, first, final = k // PJ, k % PJ == 0, k % PJ == PJ - 1
                    if first and (j or gr.beyond(1)):
                        pe.wait_ge(yT_copied, gr.count(J, j))
                    if k % 2 == 0:
                        pe.wait_ge(cmul_dve, gr.count(SLOTS, k // 2 + 1))
                    else:
                        pe.wait_ge(cmul_pool, gr.count(SLOTS, k // 2 + 1))
                    for n in range(2):
                        for t in range(TT):
                            last = turn(yT[:, j % 2, t, :], pr[:, k % 4, n, t * P:(t + 1) * P],
                                        first and n == 0 and t == 0, final and n == 1)
                    last.then_inc(summed, 1)

                work_of = [
                    (0, "S", lambda: skip(0)),
                    (2, "T", lambda: (down(e, 4), up(e, 6))),
                    (2, "F", lambda: y_back(f, qar, 3)),
                    (3, "T", lambda: gate(e, 6)),
                    (4, "F", lambda: out_proj()),
                    (5, "S", lambda: skip(1)),
                    (6, "T", lambda: (spread(e, 6), down(e, 5))),
                    (7, "F", lambda: x1_turn()),
                    (9, "P", lambda: xnorm_turn()),
                    (10, "F", lambda: (router(), gate(f, 0))),
                    (11, "F", lambda: up(f, 0)),
                    (12, "P", lambda: in_proj(0)),
                    (12, "T", lambda: down(e, 6)),
                    (12, "F", lambda: gate(f, 1)),
                    (13, "F", lambda: comb_turn()),
                    (13, "P", lambda: in_proj(1)),
                    (15, "F", lambda: up(f, 1)),
                    (17, "S", lambda: y_back(g, par, 0)),
                    (18, "F", lambda: (gate(f, 2), spread(f, 0), up(f, 2))),
                    (20, "F", lambda: gate(f, 3)),
                    (20, "P", lambda: d1()),
                    (20, "S", lambda: y_back(g, par, 1)),
                    (21, "P", lambda: d2(0)),
                    (21, "F", lambda: spread(f, 1)),
                    (22, "F", lambda: down(f, 0)),
                    (23, "P", lambda: d2(1)),
                    (24, "F", lambda: spread(f, 2)),
                    (25, "F", lambda: (up(f, 3), spread(f, 3), down(f, 1))),
                    (26, "F", lambda: gate(f, 4)),
                    (27, "S", lambda: y_back(g, par, 2)),
                    (27, "F", lambda: up(f, 4)),
                    (28, "F", lambda: down(f, 2)),
                    (29, "F", lambda: (spread(f, 4), down(f, 3), gate(f, 5))),
                    (30, "F", lambda: (spread(f, 5), up(f, 5))),
                ]
                for s in range(2 * SLOTS):
                    for half, stage, do in work_of:
                        if half == s and any(c in has for c in stage):
                            do()
                    if "S" in has and s >= 2:
                        sum_states(g, s - 2)
                    if "F" in has and s < 2:
                        sum_states(f, PAIRS - 2 + s)

            pe.wait_ge(w0_in, 16 * 5)
            run(pe, body)

        @block.scalar
        def _(act):
            af = nc.scalar.activation
            for dst, src in ((wxin, w_xin), (idn, ident), (normw, norm_w), (convw, conv_w), (convb, conv_b)):
                act.dma_start(dst[:], src).then_inc(w0_in, 16)
            act.wait_ge(prep, PREP)

            def body(g, par):
                has, q, f, e = stages(g), g + 1, g + -1, g + -2
                qar = 1 - par

                def exp_alog():
                    if g.it is None and g.base == -1:
                        act.wait_ge(w_in, 16 * 7)
                        af(amat[:], amat[:], ACT.Exp).then_inc(prep_act, 1)

                def mean_square():
                    act.wait_ge(xr_in, q.count(16, 16))
                    for t in range(TT):
                        if t or g.base >= 0:
                            act.wait_ge(squares, q.count(2, t))
                        af(sqd[:], xr[:, t, :], ACT.Square, scale=float(D) ** -0.5,
                           accum_out=mv[:, 0, t, 1:2]).then_inc(squares, 1)

                def take_roots():
                    if "P" in has:
                        act.wait_ge(squares, q.count(2, 2))
                    if "F" in has:
                        act.wait_ge(ln1_stat, f.count(4, 4))
                    af(root[:, 0:2, :], mv[:, 0:2, :, 1], ACT.Sqrt, bias=eps[:]).then_inc(roots, 1)

                def normalise():
                    act.wait_ge(inverses, g.count(1, 2))
                    for t in range(TT):
                        af(xr[:, t, :], xr[:, t, :], ACT.Copy, scale=inv[:, 0, t:t + 1]).then_inc(xn_done, 1)

                def copy_xnT():
                    act.wait_ge(xnT_ps, q.count(1, 1))
                    if "S" in has:
                        act.wait_ge(skip_ps, g.count(2, 2))
                    w = bank("xnT")[:].rearrange("p (k t) -> p k t", k=KD)
                    for k in range(KD):
                        af(xnT[:, k, :], w[:, k, :], ACT.Copy, scale=normw[:, k:k + 1]).then_inc(xnT_done, 1)

                def conv_first(i):
                    act.wait_ge(in_ps, q.count(2, i + 1))
                    if i == 0 and g.base >= 0:
                        act.wait_ge(dlt_done, q.count(1, 0))
                    w = bank(f"in{i}")[:].rearrange("p (h t) -> p h t", h=2)
                    for h in range(2):
                        j = 2 * i + h
                        af(xin[:, j, TAPS - 1:], w[:, h, :], ACT.Copy).then_inc(conv_in, 1)
                        af(xa[:, qar, j, :], w[:, h, :], ACT.Identity, bias=convb[:, j:j + 1],
                           scale=convw[:, j, TAPS - 1:TAPS]).then_inc(conv_in, 1)

                def conv_sig():
                    act.wait_ge(conv_step, q.count(12, 12))
                    af(spz[:], xa[:, qar], ACT.Tanh).then_inc(conv_tanh, 1)

                def copy_d1():
                    act.wait_ge(d1_ps, q.count(1, 1))
                    if g.base >= 0:
                        act.wait_ge(bc_st, q.count(16, 0))
                    w = bank("d1")
                    af(r1[:], w[:, 0:L], ACT.Copy).then_inc(d1_read, 1)
                    af(bcs[:], w[0:2 * NS, L:2 * L], ACT.Copy).then_inc(d1_read, 1)

                def softplus_parts(i):
                    act.wait_ge(d2_ps, q.count(2, i + 1))
                    if i == 0:
                        act.wait_ge(xa_done, q.count(1, 1))
                        if g.base >= 0:
                            act.wait_ge(dbx_full, g.count(SLOTS, 0))
                    w = bank(f"d2_{i}")[:].rearrange("p (h t) -> p h t", h=2)
                    for h in range(2):
                        j = 2 * i + h
                        af(spz[:, j, :], w[:, h, :], ACT.Abs, bias=bd2[:, j:j + 1]).then_inc(d2_read, 1)
                        af(dx[:, qar, j, :], w[:, h, :], ACT.Relu, bias=bd2[:, j:j + 1]).then_inc(d2_read, 1)

                def softplus_exp():
                    act.wait_ge(d2_read, q.count(8, 8))
                    af(spz[:], spz[:], ACT.Exp, scale=-1.0).then_inc(sp_exp, 1)

                def softplus_log():
                    act.wait_ge(sp_exp, q.count(1, 1))
                    af(dlt[:, qar], spz[:], ACT.Ln, bias=1.0).then_inc(sp_ln, 1)

                def skip_sig(i):
                    act.wait_ge(skip_ps, g.count(2, i + 1))
                    if "F" in has:
                        act.wait_ge(yg_done, f.count(J, 2 * i + 2))
                    af(sk[:, 2 * i:2 * i + 2, :], bank(f"skip{i}")[:].rearrange("p (h t) -> p h t", h=2), ACT.Tanh,
                       scale=0.5).then_inc(skip_tanh, 1)

                def copy_yT(gr, j):
                    act.wait_ge(summed, gr.count(PAIRS, PJ * (j + 1)))
                    if j >= 2 or gr.beyond(1):
                        act.wait_ge(yb_ps, gr.count(J, j - 1))
                    af(yTs[:, j % 2], yT[:, j % 2], ACT.Copy).then_inc(yT_copied, 1)

                def decay(k):
                    j, m = k // PJ, k % 2
                    if k == 0:
                        if g.it is None and g.base == 0:
                            act.wait_ge(prep_act, 2)
                        act.wait_ge(dlt_done, g.count(1, 1))
                    if k >= 2 or g.beyond(1):
                        act.wait_ge(scan_done, g.count(PAIRS, k - 1))
                    for n in range(2):
                        ns = 2 * (k % PJ) + n
                        ins = af(dA[m][:, n, 1:], dlt[:, par, j, 1:], ACT.Exp,
                                 scale=amat[:, j, ns:ns + 1])
                    ins.then_inc(dA_full, 1)

                def take_root2():
                    act.wait_ge(ln2_stat, e.count(4, 4))
                    af(root[:, 2, :], mv[:, 2, :, 1], ACT.Sqrt, bias=eps[:]).then_inc(ln2_root, 1)

                def copy_x1T():
                    act.wait_ge(x1T_ps, f.count(1, 1))
                    af(x1Th[:].rearrange("p k t -> p (k t)"), bank("x1T")[:], ACT.Copy).then_inc(x1T_done, 1)

                def route_exp():
                    act.wait_ge(rt1, f.count(2, 2))
                    af(ex[:], ex[:], ACT.Exp).then_inc(rt_exp, 1)
                    w = bank("lg")[:, 0:TT * NXS].rearrange("p (t x) -> p t x", t=TT)
                    af(sgt[:], w[:, :, NX:NXS], ACT.Tanh, scale=0.5).then_inc(rt_exp, 1)

                def copy_cT():
                    act.wait_ge(cT_ps, f.count(1, 1))
                    af(cT[:], bank("cT")[:].bitcast(BF16)[0:3 * NXS, 0:L], ACT.Copy).then_inc(cT_done, 1)

                def gate_sig(f, i):
                    act.wait_ge(g_ps, f.count(FPAIRS, i + 1))
                    if i >= HRING:
                        act.wait_ge(dn_ps, f.count(FPAIRS, i - HRING + 1))
                    elif f.beyond(1):
                        held = max(n for n in range(FPAIRS) if n % HRING == i)
                        act.wait_ge(dn_ps, f.count(FPAIRS, held + 1 - FPAIRS))
                    af(hh[:, i % HRING], gps[:], ACT.Tanh, scale=0.5).then_inc(g_tanh, 1)

                work_of = [
                    (0, "T", lambda: gate_sig(e, 5)),
                    (0, "S", lambda: skip_sig(0)),
                    (2, "F", lambda: copy_yT(f, 3)),
                    (5, "T", lambda: gate_sig(e, 6)),
                    (5, "P", lambda: mean_square()),
                    (8, "PF", lambda: take_roots()),
                    (9, "S", lambda: skip_sig(1)),
                    (9, "P", lambda: normalise()),
                    (9, "F", lambda: copy_x1T()),
                    (12, "S", lambda: copy_yT(g, 0)),
                    (12, "F", lambda: route_exp()),
                    (13, "P", lambda: copy_xnT()),
                    (14, "F", lambda: gate_sig(f, 0)),
                    (14, "P", lambda: conv_first(0)),
                    (15, "F", lambda: gate_sig(f, 1)),
                    (16, "F", lambda: copy_cT()),
                    (16, "P", lambda: conv_first(1)),
                    (17, "P", lambda: exp_alog()),
                    (18, "P", lambda: conv_sig()),
                    (19, "S", lambda: copy_yT(g, 1)),
                    (19, "F", lambda: gate_sig(f, 2)),
                    (22, "P", lambda: copy_d1()),
                    (23, "F", lambda: gate_sig(f, 3)),
                    (24, "P", lambda: softplus_parts(0)),
                    (25, "P", lambda: (softplus_parts(1), softplus_exp())),
                    (26, "S", lambda: copy_yT(g, 2)),
                    (28, "F", lambda: gate_sig(f, 4)),
                    (31, "P", lambda: softplus_log()),
                    (31, "T", lambda: take_root2()),
                ]
                for s in range(2 * SLOTS):
                    for half, stage, do in work_of:
                        if half == s and any(c in has for c in stage):
                            do()
                    if "S" in has:
                        decay(s)

            run(act, body)

        @block.gpsimd
        def _(pool):
            def body(g, par):
                has, q = stages(g), g + 1
                qar = 1 - par

                def softplus_loss():
                    pool.wait_ge(sp_low, q.count(1, 1))
                    nc.gpsimd.tensor_tensor(spu, spz[:], spu, ALU.subtract).then_inc(sp_pool, 1)

                def softplus_positive():
                    pool.wait_ge(sp_pool, q.count(2, 1))
                    nc.gpsimd.tensor_tensor(spu, dx[:, qar], spu, ALU.add).then_inc(sp_pool, 1)

                def drive(gr, gpar, c):
                    j, qd = c // NQ, c % NQ
                    if c == 0:
                        pool.wait_ge(dx_done, gr.count(1, 1))
                    if j == 0:
                        pool.wait_ge(b_in[qd], gr.count(16, 16))
                    if c >= DRING or gr.beyond(1):
                        pool.wait_ge(scan_done, gr.count(PAIRS, 2 * (c - DRING + 1)))
                    nc.gpsimd.tensor_tensor(
                        dbx[:, c % DRING], dx[:, gpar, j, :].unsqueeze(1).broadcast_to([P, QUAD, L]),
                        Bb[:, qd * QUAD:(qd + 1) * QUAD, :], ALU.mult).then_inc(dbx_full, 1)

                def weigh(gr, c):
                    k, qd = 2 * c + 1, c % NQ
                    pool.wait_ge(scan_done, gr.count(PAIRS, k + 1))
                    if c < NQ:
                        pool.wait_ge(c_in[qd], gr.count(16, 16))
                    nc.gpsimd.tensor_tensor(pr[:, k % 4], pr[:, k % 4],
                                            Cb[:, qd * QUAD + 2:(qd + 1) * QUAD, :], ALU.mult)\
                        .then_inc(cmul_pool, 1)

                work_of = [
                    (25, "P", lambda: softplus_loss()),
                    (28, "P", lambda: softplus_positive()),
                ]
                for s in range(2 * SLOTS):
                    for half, stage, do in work_of:
                        if half == s and any(c in has for c in stage):
                            do()
                    if "S" in has and s % 2 == 0 and s < 2 * SLOTS - 2:
                        drive(g, par, s // 2 + 1)
                    if "S" in has and s % 2:
                        weigh(g, s // 2)
                if "P" in has:
                    drive(q, qar, 0)

            run(pool, body)

        @block.vector
        def _(dve):
            ts, tt, stt = nc.vector.tensor_scalar, nc.vector.tensor_tensor, nc.vector.scalar_tensor_tensor
            nc.vector.memset(xin[:, :, 0:TAPS - 1], 0.0).then_inc(prep, 1)
            for i in range(2):
                nc.vector.memset(dA[i][:, :, 0:1], 0.0).then_inc(prep, 1)
            nc.vector.memset(eps[:], EPS).then_inc(prep, 1)
            nc.vector.memset(mv[:], 1.0).then_inc(prep, 1)
            dve.wait_ge(w0_in, 16 * 5)
            ts(convw[:], convw[:], 0.5, None, ALU.mult).then_inc(prep, 1)
            ts(convb[:], convb[:], 0.5, None, ALU.mult).then_inc(prep, 1)

            def negate_a():
                dve.wait_ge(w_in, 16 * 7)
                ts(wout[:], wout[:], 0.5, None, ALU.mult).then_inc(prep_wout, 1)
                dve.wait_ge(w0_in, 16 * 5)
                nc.vector.tensor_copy(idb[:], idn[:]).then_inc(prep_wout, 1)
                dve.wait_ge(prep_act, 1)
                ts(amat[:], amat[:], -1.0, None, ALU.mult).then_inc(prep_act, 1)

            def body(g, par):
                has, q, f, e = stages(g), g + 1, g + -1, g + -2
                qar = 1 - par

                def invert():
                    dve.wait_ge(roots, g.count(1, 2))
                    nc.vector.reciprocal(inv[:, 0:2, :], root[:, 0:2, :]).then_inc(inverses, 1)

                def conv(i):
                    for tap in range(TAPS - 1):
                        for h in range(2):
                            j = 2 * i + h
                            n = 6 * i + 2 * tap + h
                            if tap == 0:
                                dve.wait_ge(conv_in, q.count(8, 2 * j + 2))
                            else:
                                dve.wait_ge(conv_step, q.count(12, n - 1))
                            stt(xa[:, qar, j, :], xin[:, j, tap:tap + L], convw[:, j, tap:tap + 1], xa[:, qar, j, :],
                                ALU.mult, ALU.add).then_inc(conv_step, 1)

                def conv_silu():
                    dve.wait_ge(conv_tanh, q.count(1, 1))
                    stt(xa[:, qar], spz[:], 1.0, xa[:, qar], ALU.add, ALU.mult).then_inc(xa_done, 1)

                def softplus_low():
                    dve.wait_ge(sp_exp, q.count(1, 1))
                    ts(spu, spz[:], 1.0, -1.0, ALU.add, ALU.add).then_inc(sp_low, 1)

                def delta():
                    dve.wait_ge(sp_ln, q.count(1, 1))
                    dve.wait_ge(sp_pool, q.count(2, 2))
                    tt(dlt[:, qar], dlt[:, qar], spu, ALU.add).then_inc(dlt_done, 1)
                    dve.wait_ge(dlt_done, q.count(1, 1))
                    tt(dx[:, qar], dlt[:, qar], xa[:, qar], ALU.mult).then_inc(dx_done, 1)

                def skip_silu(i):
                    dve.wait_ge(skip_tanh, g.count(2, i + 1))
                    stt(sk[:, 2 * i:2 * i + 2, :], sk[:, 2 * i:2 * i + 2, :], 1.0,
                        bank(f"skip{i}")[:].rearrange("p (h t) -> p h t", h=2),
                        ALU.add, ALU.mult).then_inc(sk_done, 1)

                def y_gate(gr, gpar, j):
                    if j == 0 and gr.beyond(1):
                        dve.wait_ge(outp_ps, gr.count(1, 0))
                    dve.wait_ge(yb_ps, gr.count(J, j + 1))
                    stt(yg[:, j, :], xa[:, gpar, j, :], wdd[:, j:j + 1], bank(f"yb{j}")[:, 0:L],
                        ALU.mult, ALU.add).then_inc(yb_read, 1)
                    dve.wait_ge(yb_read, gr.count(J, j + 1))
                    tt(yg[:, j, :], yg[:, j, :], sk[:, j, :], ALU.mult).then_inc(yg_done, 1)

                def split_x1():
                    dve.wait_ge(x1T_done, f.count(1, 1))
                    tt(x1Tl[:], bank("x1T")[:].rearrange("p (k t) -> p k t", k=KD), x1Th[:].bitcast(F32),
                       ALU.subtract).then_inc(x1T_low, 1)

                def res_norm_stats():
                    dve.wait_ge(outp_ps, f.count(1, 1))
                    dve.wait_ge(res_in, f.count(16, 16))
                    stt(x1[:, qar], x1[:, qar], 2.0, bank("outp")[:].rearrange("p (t d) -> p t d", t=TT),
                        ALU.mult, ALU.add).then_inc(res_sum, 1)
                    dve.wait_ge(res_sum, f.count(1, 1))
                    for t in range(TT):
                        nc.vector.bn_stats(st1[:, t, :], x1[:, qar, t, :]).then_inc(ln1_stat, 1)
                    for t in range(TT):
                        need = f.held(dve, 4, t + 1)
                        dve.wait_ge(prep, PREP)
                        dve.wait_ge(ln1_stat, need)
                        nc.vector.bn_aggr(mv[:, 1, t, :], st1[:, t, :]).then_inc(ln1_stat, 1)

                def res_norm():
                    dve.wait_ge(inverses, g.count(1, 2))
                    for t in range(TT):
                        ts(x1[:, qar, t, :], x1[:, qar, t, :], mv[:, 1, t, 0:1], inv[:, 1, t:t + 1],
                           ALU.subtract, ALU.mult).then_inc(x1_done, 1)

                def route_max():
                    dve.wait_ge(lg_ps, f.count(1, 1))
                    lg = bank("lg")[:, 0:TT * NXS].rearrange("p (t x) -> p t x", t=TT)[:, :, 0:NX]
                    nc.vector.tensor_reduce(lmax[:], lg, AX.X, ALU.max).then_inc(rt1, 1)
                    dve.wait_ge(rt1, f.count(2, 1))
                    tt(ex[:], lg, lmax[:].unsqueeze(2).broadcast_to([P, TT, NX]), ALU.subtract).then_inc(rt1, 1)

                def route_top2():
                    step = [0]

                    def then(ins):
                        step[0] += 1
                        ins.then_inc(rt2, 1)

                    def settle():
                        dve.wait_ge(rt2, f.count(RT2, step[0]))

                    other = ex[:].unsqueeze(2).broadcast_to([P, TT, NX, NX])
                    own = ex[:].unsqueeze(3).broadcast_to([P, TT, NX, NX])
                    dve.wait_ge(rt_exp, f.count(2, 2))
                    then(tt(gt[:], other, own, ALU.is_gt))
                    then(tt(eq[:], other, own, ALU.is_equal))
                    settle()
                    then(tt(eq[:], eq[:], lower[:].unsqueeze(1).broadcast_to([P, TT, NX, NX]), ALU.mult))
                    settle()
                    then(tt(gt[:], gt[:], eq[:], ALU.add))
                    settle()
                    then(nc.vector.tensor_reduce(rank, gt[:], AX.X, ALU.add))
                    settle()
                    then(stt(top[:], rank, 2.0, ex[:], ALU.is_lt, ALU.mult))
                    settle()
                    then(nc.vector.tensor_reduce(tsum[:], top[:], AX.X, ALU.add))
                    settle()
                    then(nc.vector.reciprocal(tinv[:], tsum[:]))
                    settle()
                    then(stt(comb[:, :, 0:NX], top[:], 0.5, tinv[:].unsqueeze(2).broadcast_to([P, TT, NX]),
                             ALU.mult, ALU.mult))
                    then(ts(comb[:, :, NX:NXS], sgt[:], 0.25, 0.25, ALU.mult, ALU.add))
                    settle()
                    then(nc.vector.tensor_copy(cpart[:, :, 0, :], comb[:]))
                    settle()
                    then(tt(crest, comb[:], cpart[:, :, 0, :], ALU.subtract))
                    settle()
                    then(nc.vector.tensor_copy(cpart[:, :, 1, :], crest))
                    settle()
                    then(tt(comb[:], crest, cpart[:, :, 1, :], ALU.subtract))
                    settle()
                    then(nc.vector.tensor_copy(cpart[:, :, 2, :], comb[:]))
                    assert step[0] == RT2

                def glu_gate(f, i):
                    dve.wait_ge(g_tanh, f.count(FPAIRS, i + 1))
                    stt(hh[:, i % HRING], hh[:, i % HRING], 1.0, gps[:], ALU.add, ALU.mult).then_inc(g_read, 1)

                def glu_up(f, i):
                    dve.wait_ge(g_read, f.count(FPAIRS, i + 1))
                    dve.wait_ge(u_ps, f.count(FPAIRS, i + 1))
                    tt(hh[:, i % HRING], hh[:, i % HRING], ups[:], ALU.mult).then_inc(u_read, 1)

                def glu_weigh(f, i):
                    dve.wait_ge(u_read, f.count(FPAIRS, i + 1))
                    dve.wait_ge(cb_ps, f.count(FPAIRS, i + 1))
                    tt(hh[:, i % HRING], hh[:, i % HRING], bank(f"cb{i}")[:].rearrange("p (h t) -> p h t", h=2),
                       ALU.mult).then_inc(h_done, 1)

                def out_stats():
                    dve.wait_ge(dn_ps, e.count(FPAIRS, FPAIRS))
                    if e.beyond(1):
                        dve.wait_ge(out_st, e.count(16, 0))
                    tt(ob[:], x1[:, par], ops[:], ALU.add).then_inc(z2_done, 1)
                    dve.wait_ge(z2_done, e.count(1, 1))
                    for t in range(TT):
                        nc.vector.bn_stats(st2[:, t, :], ob[:, t, :]).then_inc(ln2_stat, 1)
                    for t in range(TT):
                        need = e.held(dve, 4, t + 1)
                        dve.wait_ge(prep, PREP)
                        dve.wait_ge(ln2_stat, need)
                        nc.vector.bn_aggr(mv[:, 2, t, :], st2[:, t, :]).then_inc(ln2_stat, 1)

                def out_norm():
                    dve.wait_ge(ln2_root, e.count(1, 1))
                    nc.vector.reciprocal(inv[:, 2, :], root[:, 2, :]).then_inc(ln2_inv, 1)
                    dve.wait_ge(ln2_inv, e.count(1, 1))
                    for t in range(TT):
                        ts(ob[:, t, :], ob[:, t, :], mv[:, 2, t, 0:1], inv[:, 2, t:t + 1],
                           ALU.subtract, ALU.mult).then_inc(out_done, 1)

                mul, add = ALU.mult, ALU.add

                def constants():
                    if g.it is None and g.base == -1:
                        negate_a()

                def split_weights(n):
                    if g.it is None and g.base == 0:
                        whi, wlo = ((wgh, wgl), (wuh, wul))[n // KD]
                        dve.wait_ge(wgu_in, 16 * (n + 1))
                        nc.vector.tensor_copy(whi[:, n % KD, :], staged).then_inc(wgu_part, 1)
                        dve.wait_ge(wgu_part, 2 * n + 1)
                        tt(wlo[:, n % KD, :], staged, whi[:, n % KD, :].bitcast(F32),
                           ALU.subtract).then_inc(wgu_part, 1)

                def scan(k):
                    c, n = k // 2, 2 * (k % 2)
                    if n == 0:
                        dve.wait_ge(dbx_full, g.count(SLOTS, c + 1))
                    dve.wait_ge(dA_full, g.count(PAIRS, k + 1))
                    if k >= 4 or g.beyond(1):
                        dve.wait_ge(summed, g.count(PAIRS, k - 3))
                    nc.vector.tensor_tensor_scan(
                        pr[:, k % 4].rearrange("p n t -> p (n t)"), dA[k % 2][:].rearrange("p n t -> p (n t)"),
                        dbx[:, c % DRING, n:n + 2, :].rearrange("p n t -> p (n t)"), 0.0, mul, add)\
                        .then_inc(scan_done, 1)

                def scan_even(c):
                    scan(2 * c)

                def scan_odd(c):
                    j, qd, k = c // NQ, c % NQ, 2 * c
                    scan(k + 1)
                    dve.wait_ge(scan_done, g.count(PAIRS, k + 1))
                    if j == 0:
                        dve.wait_ge(c_in[qd], g.count(16, 16))
                    tt(pr[:, k % 4], pr[:, k % 4], Cb[:, qd * QUAD:qd * QUAD + 2, :], mul).then_inc(cmul_dve, 1)

                work_of = [
                    (0, "T", lambda: (glu_gate(e, 5), glu_up(e, 5), glu_weigh(e, 5))),
                    (0, "S", lambda: skip_silu(0)),
                    (2, "S", lambda: split_weights(0)),
                    (3, "F", lambda: y_gate(f, qar, 3)),
                    (4, "T", lambda: glu_gate(e, 6)),
                    (6, "F", lambda: res_norm_stats()),
                    (6, "S", lambda: split_weights(1)),
                    (7, "T", lambda: glu_up(e, 6)),
                    (8, "PF", lambda: invert()),
                    (8, "F", lambda: res_norm()),
                    (8, "T", lambda: glu_weigh(e, 6)),
                    (8, "S", lambda: skip_silu(1)),
                    (9, "F", lambda: split_x1()),
                    (11, "F", lambda: route_max()),
                    (12, "F", lambda: (route_top2(), glu_gate(f, 0))),
                    (14, "P", lambda: conv(0)),
                    (14, "F", lambda: glu_up(f, 0)),
                    (15, "F", lambda: glu_gate(f, 1)),
                    (16, "P", lambda: conv(1)),
                    (17, "F", lambda: glu_up(f, 1)),
                    (18, "S", lambda: y_gate(g, par, 0)),
                    (18, "F", lambda: glu_gate(f, 2)),
                    (18, "P", lambda: conv_silu()),
                    (20, "F", lambda: glu_weigh(f, 0)),
                    (20, "S", lambda: split_weights(2)),
                    (20, "T", lambda: out_stats()),
                    (21, "S", lambda: y_gate(g, par, 1)),
                    (22, "F", lambda: (glu_up(f, 2), glu_weigh(f, 1))),
                    (24, "F", lambda: (glu_weigh(f, 2), glu_gate(f, 3))),
                    (25, "P", lambda: softplus_low()),
                    (25, "F", lambda: (glu_up(f, 3), glu_weigh(f, 3))),
                    (26, "S", lambda: split_weights(3)),
                    (28, "F", lambda: glu_gate(f, 4)),
                    (29, "F", lambda: glu_up(f, 4)),
                    (29, "S", lambda: y_gate(g, par, 2)),
                    (30, "F", lambda: glu_weigh(f, 4)),
                    (30, "P", lambda: delta()),
                    (31, "T", lambda: out_norm()),
                    (31, "P", lambda: constants()),
                ]
                for s in range(2 * SLOTS):
                    for half, stage, do in work_of:
                        if half == s and any(c in has for c in stage):
                            do()
                    if "S" in has:
                        (scan_odd if s % 2 else scan_even)(s // 2)

            run(dve, body)


_OUT = (16, 256, 256)


def kernel(**inputs):
    import ml_dtypes
    import numpy as np
    import concourse.bacc as _bacc
    from concourse import mybir as _mybir
    from concourse.bass_utils import run_bass_kernel_spmd as _run

    a = {k: np.asarray(v) for k, v in inputs.items()}
    P = 128

    def rows(w):
        n = w.shape[0] // P
        return np.ascontiguousarray(w.reshape(n, P, -1).swapaxes(0, 1))

    attn = lambda n: a["L0_attn_" + n]
    ffn = lambda n: a["L0_ffn_" + n]
    NX, D, H = ffn("w_gate").shape
    HS = ffn("shw_gate").shape[1]
    FEAT = NX * H + HS
    owner = np.concatenate([np.repeat(np.arange(NX), H), np.full(HS, NX)])
    sel = (owner[None, :] == (np.arange(3 * (NX + 1)) % (NX + 1))[:, None]).astype(np.float32)
    tri = np.ascontiguousarray(np.broadcast_to(np.tril(np.ones((NX, NX), np.float32), -1), (P, NX, NX)))
    side = lambda w, sh: np.concatenate([w.transpose(1, 0, 2).reshape(D, NX * H), sh], axis=1)
    arrays = {
        "resid": attn("resid"),
        "w_xin": rows(np.concatenate([attn("W_in"), attn("W_skip")], axis=0).T),
        "norm_w": rows(attn("norm_w"))[:, :, 0],
        "conv_w": rows(attn("conv_w")),
        "conv_b": rows(attn("conv_b"))[:, :, 0],
        "w_d1": rows(attn("W_d1").T),
        "w_d2": attn("W_d2").T,
        "b_d2": rows(attn("b_d2"))[:, :, 0],
        "w_bc": rows(np.concatenate([attn("W_Bm"), attn("W_Cm")], axis=0).T),
        "a_log": rows(attn("A_log")),
        "w_dd": rows(attn("W_D"))[:, :, 0],
        "w_out": rows(attn("W_out").T),
        "w_router": rows(np.concatenate([ffn("gate_w"), ffn("shgate_w")[None, :]], axis=0).T),
        "w_gate": rows(side(ffn("w_gate"), ffn("shw_gate"))),
        "w_up": rows(side(ffn("w_up"), ffn("shw_up"))),
        "w_down": np.concatenate([ffn("w_down").reshape(NX * H, D), ffn("shw_down")], axis=0),
        "sel": sel.astype(ml_dtypes.bfloat16),
        "tri": tri,
        "ident": np.eye(P, dtype=np.float32),
    }
    arrays = {f"{k}_dram": np.ascontiguousarray(v) for k, v in arrays.items()}
    nc = _bacc.Bacc("TRN2", target_bir_lowering=False, num_devices=1)
    args = [nc.dram_tensor(k, v.shape, _mybir.dt.from_np(v.dtype), kind="ExternalInput").ap()
            for k, v in arrays.items()]
    args.append(nc.dram_tensor("out_dram", _OUT, _mybir.dt.float32, kind="ExternalOutput").ap())
    build(nc, *args)
    r = _run(nc, [arrays], core_ids=[0])
    return r.results[0]["out_dram"]
```
